# Optimizing a Trainium2 kernel written in Bass

```python
import numpy as np
import jax
import jax.numpy as jnp

def _softmax(x, axis=-1):
    return jax.nn.softmax(x, axis=axis)

def _gelu(x):
    return jax.nn.gelu(x, approximate=True)

def _silu(x):
    return jax.nn.silu(x)

def _sigmoid(x):
    return jax.nn.sigmoid(x)

def _layernorm(x, axis=-1, eps=1e-05):
    m = jnp.mean(x, axis=axis, keepdims=True)
    v = jnp.var(x, axis=axis, keepdims=True)
    return (x - m) / jnp.sqrt(v + eps)

def _scatter_add(tgt, idx, src, axis=0):
    return tgt.at[idx].add(src)

def _segment_sum(src, seg, n):
    return jax.ops.segment_sum(src, seg, n)
kernel_name = 'mk_flamingo_gated_d1_seqx_r4_60c537'

def setup_inputs(seed: int=0):
    np.random.seed(seed)
    _w = jnp.asarray

    def _rec_inputs():
        import jax
        import jax.numpy as jnp
        _rk = jax.random.key(seed)
        x = -0.0002928 + 1 * jax.random.normal(jax.random.fold_in(_rk, 1), (4, 512, 256), jnp.float32)
        _lenS = 512 - jax.random.randint(jax.random.fold_in(_rk, 7), (4,), 0, max(1, 512 // 4) + 1, jnp.int32)
        _lenS2 = 512 - jax.random.randint(jax.random.fold_in(_rk, 8), (4,), 0, max(1, 512 // 4) + 1, jnp.int32)
        _ctx_512P = jax.random.normal(jax.random.fold_in(_rk, 11), (4, 16, 128), jnp.float32)
        _ctx_512c = jax.random.dirichlet(jax.random.fold_in(_rk, 511), 0.3 * jnp.ones((16,), jnp.float32), (4, 512))
        _ctx_512t = jnp.einsum('bsk,bkd->bsd', _ctx_512c, _ctx_512P)
        _ctx_512t = _ctx_512t * jax.lax.rsqrt(jnp.mean(jnp.square(_ctx_512t)) + 1e-12) * 0.953939
        ctx_512 = 0.00222621 + 0.99962 * (_ctx_512t + 0.3 * jax.random.normal(jax.random.fold_in(_rk, 611), (4, 512, 128), jnp.float32))
        _g = jax.random.normal(jax.random.fold_in(_rk, 9001), (2, 1), jnp.float32)
        _g = jnp.sign(_g) * jnp.maximum(jnp.abs(_g), 1.0) + (_g == 0) * 1.0
        g_xattn = _g[0]
        g_ffn = _g[1]
        return (x, ctx_512, g_xattn, g_ffn)
    x, ctx_512, g_xattn, g_ffn = _rec_inputs()

    def _L0_xattn_setup():
        import jax, jax.numpy as jnp
        import numpy as np
        B, T, TC, C, CC, H = (2, 512, 128, 256, 128, 16)
        D = C // H

        def _heads(t):
            b, l, _ = t.shape
            return t.reshape(b, l, H, D).transpose(0, 2, 1, 3)
        key = jax.random.key(seed)
        ks = jax.random.split(key, 18)
        w = lambda k, i, o: jax.random.normal(k, (i, o), jnp.float32) / np.sqrt(i).astype(np.float32)
        return {'x': jax.random.normal(ks[0], (B, T, C), jnp.float32), 'cross_input': jax.random.normal(ks[1], (B, TC, CC), jnp.float32), 'Wk': w(ks[2], C, C), 'bk': jnp.zeros((C,), jnp.float32), 'Wq': w(ks[3], C, C), 'bq': jnp.zeros((C,), jnp.float32), 'Wv': w(ks[4], C, C), 'bv': jnp.zeros((C,), jnp.float32), 'Wck': w(ks[5], CC, C), 'bck': jnp.zeros((C,), jnp.float32), 'Wcq': w(ks[6], C, C), 'bcq': jnp.zeros((C,), jnp.float32), 'Wcv': w(ks[7], CC, C), 'bcv': jnp.zeros((C,), jnp.float32), 'Wp': w(ks[8], C, C), 'bp': jnp.zeros((C,), jnp.float32)}
    _L0_xattn_all = _L0_xattn_setup()
    _L0_xattn_in = {k: v for k, v in _L0_xattn_all.items() if k in ('Wk', 'bk', 'Wq', 'bq', 'Wv', 'bv', 'Wck', 'bck', 'Wcq', 'bcq', 'Wcv', 'bcv', 'Wp', 'bp')}
    del _L0_xattn_all

    def _L0_ffn_setup():
        import jax, jax.numpy as jnp
        import numpy as np
        D_MODEL, FF_DIM = (256, 512)
        N_SHARED, N_ROUTED, TOP_K = (1, 8, 2)
        BATCH, SEQ = (2, 512)
        key = jax.random.key(seed)
        ks = jax.random.split(key, 8)
        init = lambda k, shape: jax.random.normal(k, shape, jnp.float32) * 0.02
        x = jax.random.normal(ks[0], (BATCH, SEQ, D_MODEL), jnp.float32)
        Wg = init(ks[1], (D_MODEL, N_ROUTED))
        Ws1 = init(ks[2], (D_MODEL, FF_DIM))
        Ws3 = init(ks[3], (D_MODEL, FF_DIM))
        Ws2 = init(ks[4], (FF_DIM, D_MODEL))
        We1 = init(ks[5], (N_ROUTED, D_MODEL, FF_DIM))
        We3 = init(ks[6], (N_ROUTED, D_MODEL, FF_DIM))
        We2 = init(ks[7], (N_ROUTED, FF_DIM, D_MODEL))
        return {'x': x, 'Wg': Wg, 'Ws1': Ws1, 'Ws3': Ws3, 'Ws2': Ws2, 'We1': We1, 'We3': We3, 'We2': We2}
    _L0_ffn_all = _L0_ffn_setup()
    _L0_ffn_in = {k: v for k, v in _L0_ffn_all.items() if k in ('Wg', 'Ws1', 'Ws3', 'Ws2', 'We1', 'We3', 'We2')}
    del _L0_ffn_all
    return {'x': x, 'ctx_512': ctx_512, 'g_xattn': g_xattn, 'g_ffn': g_ffn, 'L0_xattn_Wk': _L0_xattn_in['Wk'], 'L0_xattn_bk': _L0_xattn_in['bk'], 'L0_xattn_Wq': _L0_xattn_in['Wq'], 'L0_xattn_bq': _L0_xattn_in['bq'], 'L0_xattn_Wv': _L0_xattn_in['Wv'], 'L0_xattn_bv': _L0_xattn_in['bv'], 'L0_xattn_Wck': _L0_xattn_in['Wck'], 'L0_xattn_bck': _L0_xattn_in['bck'], 'L0_xattn_Wcq': _L0_xattn_in['Wcq'], 'L0_xattn_bcq': _L0_xattn_in['bcq'], 'L0_xattn_Wcv': _L0_xattn_in['Wcv'], 'L0_xattn_bcv': _L0_xattn_in['bcv'], 'L0_xattn_Wp': _L0_xattn_in['Wp'], 'L0_xattn_bp': _L0_xattn_in['bp'], 'L0_ffn_Wg': _L0_ffn_in['Wg'], 'L0_ffn_Ws1': _L0_ffn_in['Ws1'], 'L0_ffn_Ws3': _L0_ffn_in['Ws3'], 'L0_ffn_Ws2': _L0_ffn_in['Ws2'], 'L0_ffn_We1': _L0_ffn_in['We1'], 'L0_ffn_We3': _L0_ffn_in['We3'], 'L0_ffn_We2': _L0_ffn_in['We2']}

def reference(x, ctx_512, g_xattn, g_ffn, L0_xattn_Wk, L0_xattn_bk, L0_xattn_Wq, L0_xattn_bq, L0_xattn_Wv, L0_xattn_bv, L0_xattn_Wck, L0_xattn_bck, L0_xattn_Wcq, L0_xattn_bcq, L0_xattn_Wcv, L0_xattn_bcv, L0_xattn_Wp, L0_xattn_bp, L0_ffn_Wg, L0_ffn_Ws1, L0_ffn_Ws3, L0_ffn_Ws2, L0_ffn_We1, L0_ffn_We3, L0_ffn_We2):
    import jax
    import jax.numpy as jnp

    def _L0_xattn_ref(x, cross_input, Wk, bk, Wq, bq, Wv, bv, Wck, bck, Wcq, bcq, Wcv, bcv, Wp, bp):
        import jax, jax.numpy as jnp
        import numpy as np
        B, T, TC, C, CC, H = (2, 512, 128, 256, 128, 16)
        D = C // H

        def _heads(t):
            b, l, _ = t.shape
            return t.reshape(b, l, H, D).transpose(0, 2, 1, 3)
        scale = np.float32(1.0 / np.sqrt(D))
        q = _heads(x @ Wq + bq)
        k = _heads(x @ Wk + bk)
        v = _heads(x @ Wv + bv)
        att = jnp.einsum('bhqd,bhkd->bhqk', q, k) * scale
        causal = jnp.tril(jnp.ones((T, T), bool))
        att = jnp.where(causal[None, None], att, -jnp.inf)
        y = jnp.einsum('bhqk,bhkd->bhqd', jax.nn.softmax(att, axis=-1), v)
        qc = _heads(x @ Wcq + bcq)
        kc = _heads(cross_input @ Wck + bck)
        vc = _heads(cross_input @ Wcv + bcv)
        attc = jnp.einsum('bhqd,bhkd->bhqk', qc, kc) * scale
        y = y + jnp.einsum('bhqk,bhkd->bhqd', jax.nn.softmax(attc, axis=-1), vc)
        y = y.transpose(0, 2, 1, 3).reshape(x.shape[0], T, C)
        return y @ Wp + bp

    def _L0_ffn_ref(x, Wg, Ws1, Ws3, Ws2, We1, We3, We2):
        import jax, jax.numpy as jnp
        import numpy as np
        D_MODEL, FF_DIM = (256, 512)
        N_SHARED, N_ROUTED, TOP_K = (1, 8, 2)
        BATCH, SEQ = (2, 512)
        B, S, d = x.shape
        E = Wg.shape[1]
        xf = x.reshape(-1, d)
        T = xf.shape[0]
        gates = jax.nn.sigmoid(xf @ Wg)
        vals, idx = jax.lax.top_k(gates, TOP_K)
        vals = vals / vals.sum(axis=-1, keepdims=True)
        w = jnp.zeros((T, E), x.dtype).at[jnp.arange(T)[:, None], idx].add(vals)
        shared = jax.nn.silu(xf @ Ws1) * (xf @ Ws3) @ Ws2
        h = jax.nn.silu(jnp.einsum('td,edf->tef', xf, We1)) * jnp.einsum('td,edf->tef', xf, We3)
        routed = jnp.einsum('tef,efd,te->td', h, We2, w)
        out = (shared + routed) / (N_SHARED + TOP_K)
        return out.reshape(B, S, d)
    x = x + jnp.tanh(g_xattn[0]) * _L0_xattn_ref(_layernorm(x, axis=-1), ctx_512, L0_xattn_Wk, L0_xattn_bk, L0_xattn_Wq, L0_xattn_bq, L0_xattn_Wv, L0_xattn_bv, L0_xattn_Wck, L0_xattn_bck, L0_xattn_Wcq, L0_xattn_bcq, L0_xattn_Wcv, L0_xattn_bcv, L0_xattn_Wp, L0_xattn_bp)
    x = x + jnp.tanh(g_ffn[0]) * _L0_ffn_ref(_layernorm(x, axis=-1), L0_ffn_Wg, L0_ffn_Ws1, L0_ffn_Ws3, L0_ffn_Ws2, L0_ffn_We1, L0_ffn_We3, L0_ffn_We2)
    return x

_drawn_inputs = setup_inputs


def setup_inputs(seed=0):
    import zlib

    import numpy as np

    out = dict(_drawn_inputs(seed))
    spreads = {'L0_xattn_bk': (0.0, 0.8),
     'L0_xattn_bq': (0.0, 0.769),
     'L0_xattn_bv': (0.0, 0.1),
     'L0_xattn_bck': (0.0, 0.8),
     'L0_xattn_bcq': (0.0, 0.512),
     'L0_xattn_bcv': (0.0, 0.1),
     'L0_xattn_bp': (0.0, 0.1)}
    factors = {'L0_ffn_Wg': 8.0,
     'L0_ffn_Ws1': 8.0,
     'L0_ffn_Ws3': 8.0,
     'L0_ffn_Ws2': 8.0,
     'L0_ffn_We1': 8.0,
     'L0_ffn_We3': 8.0,
     'L0_ffn_We2': 8.0}
    for name, (base, spread) in spreads.items():
        noise = np.random.default_rng([zlib.crc32(name.encode()), seed]).standard_normal(out[name].shape)
        drawn = base * np.exp(spread * noise) if base else spread * noise
        out[name] = jnp.asarray(drawn.astype(out[name].dtype))
    for name, factor in factors.items():
        out[name] = (out[name] * factor).astype(out[name].dtype)
    return out
```

```python
from contextlib import ExitStack

import concourse.bass as bass
from concourse import mybir

F32 = mybir.dt.float32
BF16 = mybir.dt.bfloat16
I32 = mybir.dt.int32
ALU = mybir.AluOpType
ACT = mybir.ActivationFunctionType
AX = mybir.AxisListType.X

P = 128
BATCH, SEQ, DM, DC = 4, 512, 256, 128
HEADS, HD = 16, 16
EXPERTS, FF, TOPK = 8, 512, 2
KT = DM // P
QT = SEQ // P
TOK = BATCH * SEQ
NTILE = TOK // P
G = 4
SLOTS = 6
ROWS = HD * SLOTS
STACKED = ROWS + 2
SCALE = float(HD) ** -0.5
EPS = 1e-5
NEG = -1e30
RTILES = (TOK * TOPK + EXPERTS * (P - 1)) // P
XW = DM + 2
FT = FF // P
TR_BANK = (0, 1, 2)
MM_BANK, MM_RING = 4, 4
A_BANK = 0
B_BANK = 4
O_BANK, MISC_BANK = 6, 7

OUTPUTS = [("split", 0, 0), ("split", 0, 1), ("split", 1, 0), ("split", 1, 1), ("value", 0, 0), ("value", 0, 1),
           ("split", 2, 0), ("split", 2, 1), ("split", 3, 0), ("split", 3, 1), ("value", 1, 0), ("value", 1, 1)]
NSPLIT = sum(o[0] == "split" for o in OUTPUTS)
NVALUE = len(OUTPUTS) - NSPLIT
SPLIT_RING = 4
Q_PARTS = (0, 0, 0, 1, 1, 2)
K_PARTS = (0, 1, 2, 0, 1, 0)


def build(nc, x, ctx_in, g_xattn, g_ffn, Wk, bk, Wq, bq, Wv, bv, Wck, bck, Wcq, bcq, Wcv, bcv, Wp, bp,
          Wg, Ws1, Ws3, Ws2, We1, We3, We2, out):
    with ExitStack() as ctx:
        def sb(name, shape, dt=F32):
            return ctx.enter_context(nc.sbuf_tensor(name, shape, dt))

        def sem(name):
            return ctx.enter_context(nc.semaphore(name))

        stacks = nc.dram_tensor("stacks", [BATCH, 4, HEADS, HD, SLOTS, SEQ], BF16).ap()
        maxrows = nc.dram_tensor("maxrows", [BATCH * G, 2, G * QT, 2, P], BF16).ap()
        shared_rows = nc.dram_tensor("shared_rows", [TOK, DM], F32).ap()
        routed_rows = nc.dram_tensor("routed_rows", [RTILES * P, XW], F32).ap()

        ps = ctx.enter_context(nc.psum_tensor("ps", [P, 8, 512], F32))

        ident = sb("ident", [P, P])
        ident_b = sb("ident_b", [P, P], BF16)
        causal = sb("causal", [P, P])
        causal_b = sb("causal_b", [P, P], BF16)
        before = sb("before", [P, P])
        before_b = sb("before_b", [P, P], BF16)
        ones_b = sb("ones_b", [P, P], BF16)
        eps_c = sb("eps_c", [P, 1])
        minus_half = sb("minus_half", [P, 1])

        bias = sb("bias", [P, 4, 2])
        rowb = sb("rowb", [P, 3, DM])
        gates_g = sb("gates_g", [P, 2])
        tanh_g = sb("tanh_g", [P, 2])
        ffn_c = sb("ffn_c", [P, 1])
        tbp = sb("tbp", [P, DM])

        xall = sb("xall", [P, NTILE, DM])
        V = sb("V", [P, BATCH, 2, QT, DM])

        NW = EXPERTS + 1
        w_words = NW * (2 * KT * FF + FT * DM)
        arena = sb("arena", [P, w_words])
        at = [0]

        def cut(words):
            at[0] += words
            assert at[0] <= w_words
            return arena[:, at[0] - words:at[0]]

        stk = cut(G * 4 * G * SEQ // 2).bitcast(BF16).rearrange("p (s t h q) -> p s t h q", s=G, t=4, h=G)
        prob_words = cut(4 * G * SEQ)
        prob = prob_words.rearrange("p (s h q) -> p s h q", s=4, h=G)
        w13 = arena[:, 0:NW * 2 * KT * FF].rearrange("p (e m k f) -> p e m k f", e=NW, m=2, k=KT)
        w2 = arena[:, NW * 2 * KT * FF:w_words].rearrange("p (e f n) -> p e f n", e=NW, f=FT)

        s2_words = 9216
        arena2 = sb("arena2", [P, s2_words])
        at2 = [0]

        def cut2(words):
            at2[0] += words
            assert at2[0] <= s2_words, at2[0]
            return arena2[:, at2[0] - words:at2[0]]

        wproj = prob_words[:, 0:4 * KT * DM].rearrange("p (w k n) -> p w k n", w=4, k=KT)
        wcross = prob_words[:, 4 * KT * DM:4 * KT * DM + 2 * DM].rearrange("p (w n) -> p w n", w=2)
        ctx_sb = prob_words[:, 4 * KT * DM + 2 * DM:4 * KT * DM + 2 * DM + NTILE * DC].rearrange(
            "p (n c) -> p n c", n=NTILE)
        wp_sb = sb("wp_sb", [P, KT, DM])
        stats = sb("stats", [P, NTILE, 6])
        mv = sb("mv", [P, NTILE, 2])
        rstd = sb("rstd", [P, NTILE])
        xn = cut2(4 * DM).rearrange("p (t c) -> p t c", t=4)
        xnT = cut2(KT * SEQ).rearrange("p (k t) -> p k t", k=KT)
        ctxT = cut2(SEQ)
        q32 = cut2(2 * SEQ).rearrange("p (r t) -> p r t", r=2)
        rest = cut2(2 * SEQ).rearrange("p (r t) -> p r t", r=2)
        parts = cut2(SPLIT_RING * 3 * SEQ // 2).bitcast(BF16).rearrange("p (r s t) -> p r s t", r=SPLIT_RING, s=3)
        ctx_b = cut2(SEQ).rearrange("p (t c) -> p t c", t=QT)
        at2[0] = 0
        vaug = cut2(2 * 8 * G * 32).rearrange("p (r v h c) -> p r v h c", r=2, v=8, h=G)
        osb = cut2(2 * SEQ).rearrange("p (y q) -> p y q", y=2)
        ynorm = cut2(2 * QT * G * HD).rearrange("p (y q h d) -> p y q h d", y=2, q=QT, h=G)
        Y = cut2(QT * DM).rearrange("p (t c) -> p t c", t=QT)
        YT = cut2(KT * SEQ).rearrange("p (k t) -> p k t", k=KT)
        recip = cut2(2 * QT * G).rearrange("p (y q h) -> p y q h", y=2, q=QT)
        at2[0] = 0
        xrow = cut2(4 * XW).rearrange("p (r c) -> p r c", r=4)
        xT = cut2(2 * KT * P).rearrange("p (r k t) -> p r k t", r=2, k=KT)
        th = cut2(2 * FF).rearrange("p (r f) -> p r f", r=2)
        gated = cut2(2 * FF).rearrange("p (r f) -> p r f", r=2)
        hid = cut2(2 * FF).rearrange("p (r f) -> p r f", r=2)
        hT = cut2(2 * FF).rearrange("p (r f t) -> p r f t", r=2, f=FT)
        yout = cut2(2 * DM).rearrange("p (r c) -> p r c", r=2)
        wg_sb = sb("wg_sb", [P, KT, EXPERTS])
        xr = V[:, :, :, :, :].rearrange("p b y q c -> p (b y q c)")[:, 0:NTILE * XW].rearrange(
            "p (n c) -> p n c", n=NTILE)
        rt = V[:, :, :, :, :].rearrange("p b y q c -> p (b y q c)")[:, NTILE * XW:]
        rat = [0]

        def rcut(words):
            rat[0] += words
            assert rat[0] <= BATCH * 2 * QT * DM - NTILE * XW
            return rt[:, rat[0] - words:rat[0]]

        NE = NTILE * EXPERTS

        def rcut3():
            return rcut(NE).rearrange("p (n e) -> p n e", n=NTILE)

        x2nT = rcut(2 * KT * P).rearrange("p (r k t) -> p r k t", r=2, k=KT)
        expz, gate, top1, top2, pick = (rcut3() for _ in range(5))
        slot_e = rcut(NE).rearrange("p (e n) -> p e n", e=EXPERTS)
        chosen_b = rcut(NE // 2).bitcast(BF16).rearrange("p (e n) -> p e n", e=EXPERTS)
        best = rcut(NTILE * 8).rearrange("p (n e) -> p n e", n=NTILE)
        order_e = rcut(EXPERTS)
        rankv = rcut3()
        firstm = rcut3()
        gsum, ginv = rcut(NTILE), rcut(NTILE)
        wts = rcut(2 * NTILE).rearrange("p (k n) -> p k n", k=2)
        slot_f = rcut(2 * NTILE).rearrange("p (k n) -> p k n", k=2)
        slot_i = rcut(2 * NTILE).bitcast(I32).rearrange("p (k n) -> p k n", k=2)
        tok_i = rcut(NTILE).bitcast(I32)
        restart = rcut(NE)
        run_tot, slot_en = rcut(NE), rcut(NE)
        ones_e, starts = rcut(EXPERTS), rcut(EXPERTS)
        NC_I = max(RTILES, NTILE, EXPERTS)
        consts_i = rcut(NC_I).bitcast(I32)
        steps = rcut(NTILE)
        over = rcut(NE).rearrange("p (e n) -> p e n", e=EXPERTS)
        ntiles = rcut(EXPERTS)
        ends = rcut(EXPERTS)
        tile_no = rcut(RTILES)
        passed = rcut(RTILES * EXPERTS).rearrange("p (t e) -> p t e", t=RTILES)
        emap_f = rcut(RTILES)
        emap = rcut(RTILES).bitcast(I32)
        pad = sb("pad", [P, XW])
        maxes = sb("maxes", [P, 2, 2, G, QT])
        mrow = sb("mrow", [2 * QT * G, 2, 2, P], BF16)

        def ahead(name, n):
            return sem(name), n

        consts_ready, small_in, proj_in, ctx_loaded = sem("consts_ready"), sem("small_in"), sem("proj_in"), sem("ctx_loaded")
        x_in = [sem(f"x_in{b}") for b in range(BATCH)]
        shared_w_in, expert_w_in = sem("shared_w_in"), sem("expert_w_in")
        tanh_ready, tbp_ready, ffn_c_ready = sem("tanh_ready"), sem("tbp_ready"), sem("ffn_c_ready")
        stats_done, aggr_done, rstd_step, xn_ready = sem("stats_done"), sem("aggr_done"), sem("rstd_step"), sem("xn_ready")
        tr_done, TR0 = ahead("tr_done", 1)
        trT_ready, TRT0 = ahead("trT_ready", 3)
        mm_done, MM0 = ahead("mm_done", 1)
        split_high, HIGH0 = ahead("split_high", 4)
        split_rest, REST0 = ahead("split_rest", 2)
        split_mid = sem("split_mid")
        split_low, LOW0 = ahead("split_low", 2)
        value_ready, VAL0 = ahead("value_ready", 2)
        parts_out = [sem(f"parts_out{r}") for r in range(SPLIT_RING)]
        PARTS0 = 16
        ctx_staged, ones_rows, vaug_clear = sem("ctx_staged"), sem("ones_rows"), sem("vaug_clear")
        stack_in = [sem(f"stack_in{g}") for g in range(G)]
        max_in = [sem(f"max_in{g}") for g in range(G)]
        a_scores = sem("a_scores")
        a_maxed, AMAX0 = ahead("a_maxed", 2)
        misc_ready, MR0 = ahead("misc_ready", 16)
        misc_free, MISC0 = ahead("misc_free", 1)
        mrow_high, mrow_ready = sem("mrow_high"), sem("mrow_ready")
        mrow_out = sem("mrow_out")
        MROW0 = 16
        v_staged = sem("v_staged")
        b_scores = sem("b_scores")
        exp_done, EXP0 = ahead("exp_done", 2)
        masked = sem("masked")
        av_done, AV0 = ahead("av_done", 16)
        o_copied, OC0 = ahead("o_copied", 1)
        recip_done = sem("recip_done")
        ynorm_ready = sem("ynorm_ready")
        y_added, YA0 = ahead("y_added", 1)
        xb_ready = sem("xb_ready")
        yT_ready = sem("yT_ready")
        x2_ready, X20 = ahead("x2_ready", 1)
        stats2_done, aggr2_done, rstd2_step, xr_ready = (sem(n) for n in ("stats2_done", "aggr2_done", "rstd2_step", "xr_ready"))
        shared_in, t2_done, x2nT_ready, logits_done, expz_ready = (
            sem(n) for n in ("shared_in", "t2_done", "x2nT_ready", "logits_done", "expz_ready"))
        pad_ready, pad_out, dummy_out = sem("pad_ready"), sem("pad_out"), sem("dummy_out")
        route_const, route_step, chosen_ready, counts_done = (
            sem(n) for n in ("route_const", "route_step", "chosen_ready", "counts_done"))
        emap_ready, slots_ready, row_tail = sem("emap_ready"), sem("slots_ready"), sem("row_tail")
        scattered = sem("scattered")
        row_in = [sem(f"row_in{r}") for r in range(4)]
        xt_done = sem("xt_done")
        xT_ready, XT0 = ahead("xT_ready", 1)
        up_done, UP0 = ahead("up_done", 2)
        tanh_done = sem("tanh_done")
        gated_ready = sem("gated_ready")
        hid_ready, HID0 = ahead("hid_ready", 2)
        ht_done = sem("ht_done")
        hT_ready, HT0 = ahead("hT_ready", 1)
        down_done, DOWN0 = ahead("down_done", 2)
        yout_ready, YO0 = ahead("yout_ready", 2)
        row_out = sem("row_out")
        ROW0 = 32
        pool_waited = sem("pool_waited")
        row_added = sem("row_added")
        add_turn, ADD0 = ahead("add_turn", 2)

        x_tiles = x.rearrange("(n p) c -> p n c", p=P)
        ctx_tiles = ctx_in.rearrange("(n p) c -> p n c", p=P)
        out_tiles = out.rearrange("(n p) c -> n p c", p=P)

        block = ctx.enter_context(nc.Block())

        def key_tile(v):
            y, j = (1, v) if v < QT else (0, v - QT)
            return y, j, (0 if y else P * j)

        def a_unit(k):
            y, r = (1, k) if k < 8 else (0, k - 8)
            qt, pair = r // 2, r % 2
            return y, qt, pair, (SEQ if y else P * (qt + 1))

        JOBS = []
        for g in range(G):
            JOBS += [("max", g)] + ([("y", g - 1, 0)] if g else []) + [("y", g, 1)]
        JOBS += [("y", G - 1, 0), ("yt",), ("z",)]

        def job(b, *what):
            n = JOBS.index(what)
            if isinstance(b, int) and b == BATCH - 1 and n > JOBS.index(("max", G - 1)):
                n -= 1
            return len(JOBS) * b + 1 + n

        @block.sync
        def _(sp):
            for b in range(BATCH):
                sp.dma_start(xall[:, 4 * b:4 * b + 4, :], x_tiles[:, 4 * b:4 * b + 4, :]).then_inc(x_in[b], 16)
            sp.dma_start(ctx_sb, ctx_tiles).then_inc(ctx_loaded, 16)
            for r in range(SPLIT_RING):
                sp.sem_inc(parts_out[r], PARTS0)
            sp.sem_inc(mrow_out, MROW0)
            sp.sem_inc(row_out, ROW0)
            sp.wait_ge(pad_ready, 1)
            sp.dma_start(routed_rows.rearrange("(t p) c -> p t c", p=P),
                         pad[:].unsqueeze(1).to_broadcast([P, RTILES, XW])).then_inc(pad_out, 16)
            sp.dma_start(out[TOK:TOK + P, :], pad[:, 0:DM]).then_inc(dummy_out, 16)

            with sp.Fori(0, BATCH) as b:
                for n in range(NSPLIT):
                    t, half, r = n // 2, n % 2, n % SPLIT_RING
                    sp.wait_ge(split_low, LOW0 + NSPLIT * b + n + 1)
                    dst = stacks[b, t, 8 * half:8 * half + 8].rearrange("h d s q -> (h d) s q")
                    at_slot = 0
                    for run in (((0, 0, 0), (1, 1), (2,)) if t % 2 == 0 else ((0, 1, 2), (0, 1), (0,))):
                        same = len(set(run)) == 1
                        src = parts[:, r, run[0]:run[0] + 1, :].to_broadcast([P, len(run), SEQ]) if same \
                            else parts[:, r, run[0]:run[-1] + 1, :]
                        sp.dma_start(dst[:, at_slot:at_slot + len(run), :], src).then_inc(parts_out[r], 16)
                        at_slot += len(run)

            per_batch = 16 * 3 * (NSPLIT // SPLIT_RING)

            def load_stack(b, g):
                for t in range(4):
                    sp.dma_start(stk[0:ROWS, g, t], stacks[b, t, G * g:G * g + G].rearrange(
                        "h d s q -> (d s) h q")).then_inc(stack_in[g], 16)

            def max_rows(u, r, g):
                sp.wait_ge(mrow_ready, u + 1)
                sp.dma_start(maxrows[u].rearrange("y c s q -> (y c) s q"), mrow[:, r]).then_inc(mrow_out, 16)
                sp.wait_ge(mrow_out, MROW0 + 16 * (u + 1))
                for y in range(2):
                    sp.dma_start(stk[ROWS:STACKED, g, 2 * y].rearrange("o h (t q) -> o (h t) q", t=QT),
                                 maxrows[u, y].rearrange("c s q -> s c q")).then_inc(max_in[g], 16)

            for r in range(SPLIT_RING):
                sp.wait_ge(parts_out[r], PARTS0 + per_batch)
            for g in range(G):
                load_stack(0, g)
            max_rows(0, 0, 0)
            for r in range(SPLIT_RING):
                sp.wait_ge(parts_out[r], PARTS0 + BATCH * per_batch)
            with sp.Fori(0, BATCH - 1) as b:
                for g in range(G):
                    max_rows(G * b + g + 1, (g + 1) % 2, (g + 1) % G)
                    sp.wait_ge(av_done, AV0 + 8 * (G * b + g) + 8)
                    load_stack(b + 1, g)
            for g in range(G - 1):
                max_rows(G * (BATCH - 1) + g + 1, (g + 1) % 2, (g + 1) % G)

            sp.wait_ge(av_done, AV0 + 8 * G * BATCH)
            for e in [EXPERTS] + list(range(EXPERTS)):
                loaded = shared_w_in if e == EXPERTS else expert_w_in
                up_a, up_b, down = (Ws1, Ws3, Ws2) if e == EXPERTS else (We1[e], We3[e], We2[e])
                sp.dma_start(w13[:, e, 0], up_a.rearrange("(k p) f -> p k f", p=P)).then_inc(loaded, 16)
                sp.dma_start(w13[:, e, 1], up_b.rearrange("(k p) f -> p k f", p=P)).then_inc(loaded, 16)
                sp.dma_start(w2[:, e], down.rearrange("(k p) n -> p k n", p=P)).then_inc(loaded, 16)

            sh = shared_rows.rearrange("(n p) c -> n p c", p=P)
            ro = routed_rows.rearrange("(n p) c -> n p c", p=P)
            for n in range(NTILE):
                sp.wait_ge(xr_ready, n + 1)
                sp.dma_start(sh[n], xr[:, n, 0:DM]).then_inc(shared_in, 16)
            sp.wait_ge(shared_in, 16 * NTILE)

            for t in range(4):
                sp.dma_start(xrow[:, t, 0:DM], sh[t]).then_inc(row_in[t], 16)
            with sp.Fori(0, NTILE // 4 - 1) as i:
                for r in range(4):
                    sp.wait_ge(yout_ready, YO0 + 4 * i + r + 1)
                    sp.dma_start(out_tiles[4 * i + r], yout[:, r % 2]).then_inc(row_out, 16)
                    sp.dma_start(xrow[:, r, 0:DM], sh[4 * i + r + 4]).then_inc(row_in[r], 16)
            for r in range(4):
                sp.wait_ge(yout_ready, YO0 + NTILE - 4 + r + 1)
                sp.dma_start(out_tiles[NTILE - 4 + r], yout[:, r % 2]).then_inc(row_out, 16)
                if r == 0:
                    sp.wait_ge(scattered, 16 * 2 * NTILE)
                sp.dma_start(xrow[:, r], ro[r]).then_inc(row_in[r], 16)
            with sp.Fori(0, (RTILES - 4) // 4) as i:
                for r in range(4):
                    sp.wait_ge(add_turn, ADD0 + 4 * i + r + 1)
                    sp.dma_start(xrow[:, r], ro[4 * i + r + 4]).then_inc(row_in[r], 16)
            for t in range((RTILES - 4) // 4 * 4 + 4, RTILES):
                sp.wait_ge(add_turn, ADD0 + t - 4 + 1)
                sp.dma_start(xrow[:, t % 4], ro[t]).then_inc(row_in[t % 4], 16)
            sp.wait_ge(row_out, ROW0 + 16 * NTILE)
            sp.wait_ge(dummy_out, 16)
            sp.wait_ge(row_added, 16 * RTILES)

        @block.scalar
        def _(act):
            for t, w in enumerate((Wq, Wk, Wcq, Wv)):
                act.dma_start(wproj[:, t], w.rearrange("(k p) n -> p k n", p=P)).then_inc(proj_in, 16)
            for t, w in enumerate((Wck, Wcv)):
                act.dma_start(wcross[:, t], w).then_inc(proj_in, 16)
            for t, v in enumerate((bq, bk, bcq, bck)):
                act.dma_start(bias[:, t], v.rearrange("(m p) -> p m", p=P),
                              allow_slow_non_contiguous=True).then_inc(small_in, 16)
            for t, v in enumerate((bv, bcv, bp)):
                act.dma_start(rowb[:, t], v.partition_broadcast(P)).then_inc(small_in, 16)
            for t, v in enumerate((g_xattn, g_ffn)):
                act.dma_start(gates_g[:, t:t + 1], v.partition_broadcast(P)).then_inc(small_in, 16)
            act.dma_start(wp_sb[:], Wp.rearrange("(k p) n -> p k n", p=P)).then_inc(small_in, 16)
            act.dma_start(wg_sb[:], Wg.rearrange("(k p) n -> p k n", p=P)).then_inc(small_in, 16)
            for s, n in ((trT_ready, TRT0), (split_high, HIGH0), (exp_done, EXP0), (o_copied, OC0), (xT_ready, XT0),
                         (hT_ready, HT0)):
                act.sem_inc(s, n)
            act.wait_ge(small_in, 16 * 11)
            act.activation(tanh_g[:], gates_g[:], ACT.Tanh).then_inc(tanh_ready, 1)

            def copy_transposes(b, k):
                act.wait_ge(tr_done, TR0 + 3 * b + k + 1)
                dst = xnT[:, k] if k < 2 else ctxT
                act.copy(dst, ps[:, TR_BANK[k]]).then_inc(trT_ready, 1)

            with act.Fori(0, BATCH) as b:
                act.wait_ge(mm_done, MM0 + len(OUTPUTS) * b)
                copy_transposes(b, 0)
                copy_transposes(b, 1)
                n = 0
                for i, (kind, t, half) in enumerate(OUTPUTS):
                    if i == 6:
                        copy_transposes(b, 2)
                    if kind == "value":
                        continue
                    r = n % SPLIT_RING
                    bank = ps[:, MM_BANK + i % MM_RING]
                    act.wait_ge(mm_done, MM0 + len(OUTPUTS) * b + i + 1)
                    act.wait_ge(split_rest, REST0 + NSPLIT * b + n - 1)
                    act.activation(q32[:, n % 2], bank, ACT.Identity,
                                   bias=bias[:, t, half:half + 1]).then_inc(split_high, 1)
                    act.wait_ge(parts_out[r], PARTS0 + 48 * (NSPLIT // SPLIT_RING * b + n // SPLIT_RING))
                    act.activation(parts[:, r, 0], bank, ACT.Identity,
                                   bias=bias[:, t, half:half + 1]).then_inc(split_high, 1)
                    n += 1

            def high_rows(b, u, r, *what):
                act.wait_ge(misc_ready, MR0 + (job(b, *what) if what else 0) + 1)
                if what:
                    act.wait_ge(mrow_out, MROW0 + 16 * (u - 1))
                act.activation(mrow[:, r, 0], ps[0:32, MISC_BANK, 0:P], ACT.Copy, scale=-1.0).then_inc(mrow_high, 1)

            def exponentials(b, g, v):
                y, j, q0 = key_tile(v)
                step = 8 * (G * b + g) + v
                act.wait_ge(av_done, AV0 + step - 3)
                for h in range(G):
                    act.wait_ge(b_scores, 4 * step + h + 1)
                    act.activation(prob[:, v % 4, h, q0:SEQ], ps[:, B_BANK + h % 2, q0:SEQ], ACT.Exp,
                                   scale=SCALE).then_inc(exp_done, 1)

            def copy_o(b, g, y):
                u = G * b + g
                act.wait_ge(av_done, AV0 + 8 * u + (4 if y else 8))
                before_job = job(b, "y", g - 1, y) if g else job(b - 1, "y", G - 1, y)
                act.wait_ge(misc_ready, MR0 + before_job + 1)
                act.copy(osb[:, y], ps[:, O_BANK]).then_inc(o_copied, 1)

            def attention_batch(b, last):
                for g in range(G):
                    for v in range(8):
                        exponentials(b, g, v)
                        if v == 0 and g > 0:
                            copy_o(b, g - 1, 0)
                        if v == 1 and not (last and g == G - 1):
                            high_rows(b, G * b + g + 1, (g + 1) % 2, "max", g)
                        if v == 4:
                            copy_o(b, g, 1)
                copy_o(b, G - 1, 0)
                act.wait_ge(misc_ready, MR0 + job(b, "yt") + 1)
                act.copy(YT[:, 0], ps[:, MISC_BANK]).then_inc(misc_free, 1)
                act.copy(YT[:, 1], ps[:, O_BANK]).then_inc(yT_ready, 1)

            high_rows(0, 0, 0)
            with act.Fori(0, BATCH - 1) as b:
                attention_batch(b, False)
            attention_batch(BATCH - 1, True)

            for n in range(NTILE):
                act.wait_ge(t2_done, n + 1)
                if n >= 2:
                    act.wait_ge(logits_done, n - 1)
                act.copy(x2nT[:, n % 2].rearrange("p k t -> p (k t)"), ps[:, n % 2, 0:DM]).then_inc(x2nT_ready, 1)
            act.wait_ge(logits_done, NTILE)
            act.activation(expz.rearrange("p n e -> p (n e)"), ps[:, 2, 0:NE], ACT.Exp, scale=-1.0).then_inc(expz_ready, 1)

            def copy_rows(t, r):
                act.wait_ge(xt_done, t + 1)
                act.wait_ge(up_done, UP0 + t - 1)
                act.copy(xT[:, r % 2].rearrange("p k t -> p (k t)"), ps[:, 0, 0:DM]).then_inc(xT_ready, 1)

            def tanh(t, r):
                act.wait_ge(up_done, UP0 + t + 1)
                act.wait_ge(hid_ready, HID0 + t - 1)
                act.activation(th[:, r % 2], ps[:, 1 + r % 2], ACT.Tanh, scale=0.5).then_inc(tanh_done, 1)

            def copy_hidden(t, r):
                act.wait_ge(ht_done, t + 1)
                act.wait_ge(down_done, DOWN0 + t - 1)
                act.copy(hT[:, r % 2].rearrange("p f t -> p (f t)"), ps[:, 5]).then_inc(hT_ready, 1)

            def routed_out(rt, r):
                act.wait_ge(down_done, DOWN0 + NTILE + rt + 1)
                act.wait_ge(add_turn, ADD0 + rt - 1)
                act.activation(yout[:, r % 2], ps[:, 6 + r % 2, 0:DM], ACT.Copy,
                               scale=xrow[:, r, DM + 1:DM + 2]).then_inc(yout_ready, 1)

            def step(t, r, todo):
                if todo >= 3:
                    copy_rows(t + 2, r + 2)
                if todo >= 2:
                    tanh(t + 1, r + 1)
                copy_hidden(t, r)

            copy_rows(0, 0)
            copy_rows(1, 1)
            tanh(0, 0)
            with act.Fori(0, NTILE // 4) as i:
                for r in range(4):
                    step(4 * i + r, r, 3)
            act.wait_ge(row_out, ROW0 + 16 * NTILE)
            with act.Fori(0, (RTILES - 2) // 4) as i:
                for r in range(4):
                    step(NTILE + 4 * i + r, r, 3)
                    routed_out(4 * i + r, r)
            for rt in range((RTILES - 2) // 4 * 4, RTILES):
                step(NTILE + rt, rt % 4, min(3, RTILES - rt))
                routed_out(rt, rt % 4)

        @block.vector
        def _(dve):
            for s, n in ((split_rest, REST0), (split_low, LOW0), (value_ready, VAL0), (a_maxed, AMAX0),
                         (misc_free, MISC0), (x2_ready, X20), (hid_ready, HID0), (yout_ready, YO0)):
                dve.sem_inc(s, n)
            dve.memset(stk[ROWS:STACKED].rearrange("p s (y t) h q -> p (s y) t (h q)", t=2)[:, :, 1, :],
                       1.0).then_inc(ones_rows, 1)
            dve.memset(eps_c[:], EPS).then_inc(ones_rows, 1)
            dve.memset(minus_half[:], -0.5).then_inc(ones_rows, 1)
            for n in range(NTILE):
                if n % 4 == 0:
                    dve.wait_ge(x_in[n // 4], 16)
                dve.bn_stats(stats[:, n], xall[:, n]).then_inc(stats_done, 1)
                if n % 4 == 3:
                    for m in range(n - 3, n + 1):
                        dve.wait_ge(stats_done, m + 1)
                        dve.bn_aggr(mv[:, m], stats[:, m]).then_inc(aggr_done, 1)
            dve.wait_ge(tanh_ready, 1)
            dve.tensor_scalar(tbp[:], rowb[:, 2], tanh_g[:, 0:1], None, ALU.mult).then_inc(tbp_ready, 1)
            dve.tensor_scalar(ffn_c[:], tanh_g[:, 1:2], 0.5 / (1 + TOPK), None, ALU.mult).then_inc(ffn_c_ready, 1)

            def low_part(b, n):
                r = n % SPLIT_RING
                dve.wait_ge(split_rest, REST0 + NSPLIT * b + n + 1)
                dve.wait_ge(split_mid, NSPLIT * b + n + 1)
                dve.tensor_tensor(parts[:, r, 2], rest[:, n % 2], parts[:, r, 1], ALU.subtract).then_inc(split_low, 1)

            with dve.Fori(0, BATCH) as b:
                dve.wait_ge(rstd_step, 2 * b + 2)
                dve.wait_ge(tr_done, TR0 + 3 * b)
                for t in range(4):
                    dve.tensor_scalar(xn[:, t], xall[:, 4 * b + t], mv[:, 4 * b + t, 0:1], rstd[:, bass.ds(4 * b + t, 1)],
                                      ALU.subtract, ALU.mult).then_inc(xn_ready, 1)
                n = m = 0
                for i, (kind, t, half) in enumerate(OUTPUTS):
                    bank = ps[:, MM_BANK + i % MM_RING]
                    if kind == "value":
                        dve.wait_ge(mm_done, MM0 + len(OUTPUTS) * b + i + 1)
                        dve.tensor_tensor(V[:, b, 1 - t, 2 * half:2 * half + 2, :],
                                          bank.rearrange("p (t c) -> p t c", t=2),
                                          rowb[:, t:t + 1].to_broadcast([P, 2, DM]), ALU.add).then_inc(value_ready, 1)
                        m += 1
                    else:
                        dve.wait_ge(split_high, HIGH0 + 2 * (NSPLIT * b + n + 1))
                        dve.wait_ge(split_low, LOW0 + NSPLIT * b + n - 1)
                        dve.tensor_tensor(rest[:, n % 2], q32[:, n % 2], parts[:, n % SPLIT_RING, 0],
                                          ALU.subtract).then_inc(split_rest, 1)
                        if n:
                            low_part(b, n - 1)
                        n += 1
                low_part(b, NSPLIT - 1)

            def unit_max(u, r, k):
                y, qt, pair, keys = a_unit(k)
                dve.wait_ge(a_scores, 16 * u + k + 1)
                slot = A_BANK + 2 * (k % 2)
                dve.tensor_reduce(maxes[:, r, y, 2 * pair:2 * pair + 2, qt], ps[:, slot:slot + 2, 0:keys], AX,
                                  ALU.max).then_inc(a_maxed, 1)

            def middle_rows(u, r):
                dve.wait_ge(mrow_high, u + 1)
                dve.scalar_tensor_tensor(out=mrow[:, r, 1], in0=ps[0:32, MISC_BANK, 0:P], scalar=-1.0, in1=mrow[:, r, 0],
                                         op0=ALU.mult, op1=ALU.subtract).then_inc(mrow_ready, 1)
                dve.wait_ge(mrow_ready, u + 1)
                dve.sem_inc(misc_free, 1)

            def normalize(b, g, y):
                u = G * b + g
                dve.wait_ge(misc_ready, MR0 + job(b, "y", g, y) + 1)
                rows = ps[:, MISC_BANK].rearrange("p (q h c) -> p q h c", q=QT, h=G)
                done = 2 * u + (1 if y else 2)
                dve.reciprocal(recip[:, y], rows[:, :, :, HD]).then_inc(recip_done, 1)
                dve.wait_ge(recip_done, done)
                dve.wait_ge(y_added, YA0 + u)
                dve.tensor_tensor(ynorm[:, y], rows[:, :, :, 0:HD],
                                  recip[:, y].unsqueeze(3).to_broadcast([P, QT, G, HD]), ALU.mult).then_inc(ynorm_ready, 1)
                dve.wait_ge(ynorm_ready, done)
                dve.sem_inc(misc_free, 1)

            def attention_batch(b, last):
                for g in range(G):
                    for v in range(8):
                        if not (last and g >= 2):
                            unit_max(G * b + g + 2, g % 2, 2 * v)
                            unit_max(G * b + g + 2, g % 2, 2 * v + 1)
                        if v == 1 and not (last and g == G - 1):
                            middle_rows(G * b + g + 1, (g + 1) % 2)
                        if v == 2 and g > 0:
                            normalize(b, g - 1, 0)
                        if v == 6:
                            normalize(b, g, 1)
                normalize(b, G - 1, 0)
                dve.wait_ge(misc_ready, MR0 + job(b, "z") + 1)
                dve.wait_ge(xb_ready, b + 1)
                for half, bank in enumerate((MISC_BANK, O_BANK)):
                    tiles = xall[:, bass.ds(4 * b + 2 * half, 2)]
                    dve.scalar_tensor_tensor(out=tiles, in0=ps[:, bank].rearrange("p (t c) -> p t c", t=2),
                                             scalar=tanh_g[:, 0:1], in1=tiles, op0=ALU.mult,
                                             op1=ALU.add).then_inc(x2_ready, 1)
                dve.wait_ge(x2_ready, X20 + 2 * b + 2)
                dve.sem_inc(misc_free, 1)

            for u in range(2):
                for k in range(16):
                    unit_max(u, u, k)
                if u == 0:
                    middle_rows(0, 0)
            with dve.Fori(0, BATCH - 1) as b:
                attention_batch(b, False)
            attention_batch(BATCH - 1, True)

            for n in range(NTILE):
                dve.bn_stats(stats[:, n], xall[:, n]).then_inc(stats2_done, 1)
            for n in range(NTILE):
                dve.wait_ge(stats2_done, n + 1)
                dve.bn_aggr(mv[:, n], stats[:, n]).then_inc(aggr2_done, 1)
            dve.wait_ge(v_staged, G * BATCH)
            for n in range(NTILE):
                dve.wait_ge(rstd2_step, 2 * (n // 4) + 2)
                dve.tensor_scalar(xr[:, n, 0:DM], xall[:, n], mv[:, n, 0:1], rstd[:, n:n + 1],
                                  ALU.subtract, ALU.mult).then_inc(xr_ready, 1)

            steps_done = [0]

            def chain(ins):
                steps_done[0] += 1
                ins.then_inc(route_step, 1)
                dve.wait_ge(route_step, steps_done[0])

            def over_e(t):
                return t.unsqueeze(2).to_broadcast([P, NTILE, EXPERTS])

            dve.wait_ge(route_const, 3)
            dve.wait_ge(expz_ready, 1)
            order_bc = order_e.unsqueeze(1).to_broadcast([P, NTILE, EXPERTS])
            chain(dve.tensor_scalar(gate, expz, 1.0, None, ALU.add))
            chain(dve.reciprocal(gate, gate))
            chain(dve.tensor_reduce(best[:, :, 0], gate, AX, ALU.max))
            chain(dve.tensor_tensor(firstm, gate, over_e(best[:, :, 0]), ALU.is_equal))
            chain(dve.tensor_tensor(rankv, firstm, order_bc, ALU.mult))
            chain(dve.tensor_reduce(best[:, :, 1], rankv, AX, ALU.max))
            chain(dve.tensor_tensor(top1, rankv, over_e(best[:, :, 1]), ALU.is_equal))
            chain(dve.scalar_tensor_tensor(out=pick, in0=top1, scalar=-2.0, in1=gate, op0=ALU.mult, op1=ALU.add))
            chain(dve.tensor_reduce(best[:, :, 2], pick, AX, ALU.max))
            chain(dve.tensor_tensor(firstm, pick, over_e(best[:, :, 2]), ALU.is_equal))
            chain(dve.tensor_tensor(rankv, firstm, order_bc, ALU.mult))
            chain(dve.tensor_reduce(best[:, :, 3], rankv, AX, ALU.max))
            chain(dve.tensor_tensor(top2, rankv, over_e(best[:, :, 3]), ALU.is_equal))
            dve.tensor_tensor(chosen_b, top1.rearrange("p n e -> p e n"), top2.rearrange("p n e -> p e n"),
                              ALU.add).then_inc(chosen_ready, 1)
            chain(dve.tensor_tensor(gsum, best[:, :, 0], best[:, :, 2], ALU.add))
            chain(dve.reciprocal(ginv, gsum))
            dve.wait_ge(ffn_c_ready, 1)
            for k in range(2):
                chain(dve.scalar_tensor_tensor(out=wts[:, k], in0=best[:, :, 2 * k], scalar=ffn_c[:, 0:1], in1=ginv,
                                               op0=ALU.mult, op1=ALU.mult))
            dve.wait_ge(counts_done, 1)
            earlier = ps[:, 7, 0:NE]
            totals = ps[:, 7, NE:2 * NE]
            chain(dve.tensor_tensor_scan(run_tot, restart, totals, 0.0, ALU.mult, ALU.add))
            run_en = run_tot.rearrange("p (e n) -> p e n", e=EXPERTS)
            chain(dve.tensor_tensor(over, run_en[:, :, NTILE - 1:NTILE].to_broadcast([P, EXPERTS, NTILE]),
                                    steps.unsqueeze(1).to_broadcast([P, EXPERTS, NTILE]), ALU.is_gt))
            chain(dve.tensor_reduce(ntiles, over, AX, ALU.add))
            chain(dve.tensor_tensor_scan(ends, ones_e, ntiles, 0.0, ALU.mult, ALU.add))
            chain(dve.tensor_tensor(passed, tile_no.unsqueeze(2).to_broadcast([P, RTILES, EXPERTS]),
                                    ends.unsqueeze(1).to_broadcast([P, RTILES, EXPERTS]), ALU.is_ge))
            chain(dve.tensor_reduce(emap_f, passed, AX, ALU.add))
            dve.tensor_scalar(emap, emap_f, float(EXPERTS - 1), None, ALU.min).then_inc(emap_ready, 1)
            chain(dve.tensor_tensor(starts, ends, ntiles, ALU.subtract))
            chain(dve.tensor_tensor(slot_en, run_tot, totals, ALU.subtract))
            chain(dve.tensor_tensor(slot_en, slot_en, earlier, ALU.add))
            slot_v = slot_en.rearrange("p (e n) -> p e n", e=EXPERTS)
            chain(dve.scalar_tensor_tensor(out=slot_e, in0=starts.unsqueeze(2).to_broadcast([P, EXPERTS, NTILE]),
                                           scalar=float(P), in1=slot_v, op0=ALU.mult, op1=ALU.add))
            for k, top in enumerate((top1, top2)):
                chain(dve.tensor_tensor(pick, top, slot_e.rearrange("p e n -> p n e"), ALU.mult))
                chain(dve.tensor_reduce(slot_f[:, k], pick, AX, ALU.add))
                dve.tensor_copy(slot_i[:, k], slot_f[:, k]).then_inc(slots_ready, 1)

            def hidden(t, r):
                a, b_ = ps[:, 1 + r % 2], ps[:, 3 + r % 2]
                dve.wait_ge(tanh_done, t + 1)
                dve.scalar_tensor_tensor(out=gated[:, r % 2], in0=th[:, r % 2], scalar=1.0, in1=a, op0=ALU.add,
                                         op1=ALU.mult).then_inc(gated_ready, 1)
                dve.wait_ge(gated_ready, t + 1)
                dve.tensor_tensor(hid[:, r % 2], gated[:, r % 2], b_, ALU.mult).then_inc(hid_ready, 1)

            def shared_out(t, r):
                dve.wait_ge(down_done, DOWN0 + t + 1)
                dve.wait_ge(row_out, ROW0 + 16 * (t - 1))
                dve.scalar_tensor_tensor(out=yout[:, r % 2], in0=ps[:, 6 + r % 2, 0:DM], scalar=ffn_c[:, 0:1],
                                         in1=xall[:, t], op0=ALU.mult, op1=ALU.add).then_inc(yout_ready, 1)

            hidden(0, 0)
            with dve.Fori(0, NTILE // 4) as i:
                for r in range(4):
                    hidden(4 * i + r + 1, r + 1)
                    shared_out(4 * i + r, r)
            with dve.Fori(0, (RTILES - 2) // 4) as i:
                for r in range(4):
                    hidden(NTILE + 4 * i + r + 1, r + 1)
            for rt in range((RTILES - 2) // 4 * 4 + 1, RTILES):
                hidden(NTILE + rt, rt % 4)

        @block.gpsimd
        def _(pool):
            for s, n in ((y_added, YA0), (add_turn, ADD0)):
                pool.sem_inc(s, n)
            pool.memset(ident[:], 0.0).then_inc(consts_ready, 1)
            pool.memset(causal[:], 0.0).then_inc(consts_ready, 1)
            pool.memset(before[:], 0.0).then_inc(consts_ready, 1)
            pool.memset(ones_b[:], 1.0).then_inc(consts_ready, 1)
            pool.memset(pad[:], 0.0).then_inc(consts_ready, 1)
            pool.wait_ge(consts_ready, 5)
            pool.affine_select(out=ident[:], in_=ident[:], compare_op=ALU.not_equal, fill=1.0, base=0,
                               pattern=[[-1, P]], channel_multiplier=1).then_inc(consts_ready, 1)
            pool.affine_select(out=causal[:], in_=causal[:], compare_op=ALU.is_ge, fill=NEG, base=0,
                               pattern=[[-1, P]], channel_multiplier=1).then_inc(consts_ready, 1)
            pool.affine_select(out=before[:], in_=before[:], compare_op=ALU.is_ge, fill=1.0, base=0,
                               pattern=[[-1, P]], channel_multiplier=1).then_inc(consts_ready, 1)
            pool.wait_ge(consts_ready, 8)
            for dst, src in ((ident_b, ident), (causal_b, causal), (before_b, before)):
                pool.tensor_scalar(dst[:], src[:], 1.0, None, ALU.mult).then_inc(consts_ready, 1)
            pool.iota(pad[:, DM:DM + 1].bitcast(I32), pattern=[[0, 1]], base=TOK, channel_multiplier=1).then_inc(pad_ready, 1)

            pool.wait_ge(ones_rows, 3)

            def alone():
                pool.sem_inc(pool_waited, 1)

            for c in range(BATCH):
                pool.wait_ge(aggr_done, 4 * (c + 1))
                pool.tensor_tensor(rstd[:, 4 * c:4 * c + 4], mv[:, 4 * c:4 * c + 4, 1],
                                   eps_c[:].to_broadcast([P, 4]), ALU.add).then_inc(rstd_step, 1)
                pool.wait_ge(rstd_step, 2 * c + 1)
                pool.tensor_tensor(rstd[:, 4 * c:4 * c + 4], rstd[:, 4 * c:4 * c + 4],
                                   minus_half[:].to_broadcast([P, 4]), ALU.pow).then_inc(rstd_step, 1)

            pool.wait_ge(ctx_loaded, 16)
            with pool.Fori(0, BATCH) as b:
                pool.wait_ge(tr_done, TR0 + 3 * b)
                pool.tensor_copy(ctx_b, ctx_sb[:, bass.ds(4 * b, 4)]).then_inc(ctx_staged, 1)
                for n in range(NSPLIT):
                    pool.wait_ge(split_rest, REST0 + NSPLIT * b + n + 1)
                    alone()
                    pool.tensor_scalar(parts[:, n % SPLIT_RING, 1], rest[:, n % 2], 1.0, None,
                                       ALU.mult).then_inc(split_mid, 1)

            pool.wait_ge(mm_done, MM0 + BATCH * len(OUTPUTS))
            pool.memset(vaug, 0.0).then_inc(vaug_clear, 1)
            pool.wait_ge(vaug_clear, 1)
            pool.memset(vaug[:, :, :, :, HD:HD + 1], 1.0).then_inc(vaug_clear, 1)
            pool.wait_ge(vaug_clear, 2)
            pool.wait_ge(value_ready, VAL0 + BATCH * NVALUE)
            pool.wait_ge(tbp_ready, 1)

            def add_types(b, g):
                u = G * b + g
                pool.wait_ge(ynorm_ready, 2 * u + 2)
                pool.wait_ge(misc_ready, MR0 + job(b - 1, "yt") + 1)
                cols = Y[:, :, G * HD * g:G * HD * (g + 1)].rearrange("p q (h d) -> p q h d", h=G)
                pool.tensor_tensor(cols, ynorm[:, 0], ynorm[:, 1], ALU.add).then_inc(y_added, 1)

            with pool.Fori(0, BATCH) as b:
                for g in range(G):
                    u = G * b + g
                    pool.wait_ge(av_done, AV0 + 8 * u - 8)
                    pool.tensor_copy(vaug[:, g % 2, :, :, 0:HD], V[:, b, :, :, G * HD * g:G * HD * (g + 1)].rearrange(
                        "p y j (h d) -> p (y j) h d", h=G)).then_inc(v_staged, 1)
                    if g > 0:
                        add_types(b, g - 1)
                    if g == 1:
                        tiles = xall[:, bass.ds(4 * b, 4)]
                        pool.tensor_tensor(tiles, tiles, tbp[:].unsqueeze(1).to_broadcast([P, 4, DM]),
                                           ALU.add).then_inc(xb_ready, 1)
                    for v in range(4, 8):
                        _y, j, q0 = key_tile(v)
                        pool.wait_ge(exp_done, EXP0 + 4 * (8 * u + v) + 4)
                        alone()
                        diag = prob[:, v % 4, :, q0:q0 + P]
                        pool.affine_select(out=diag, in_=diag, compare_op=ALU.is_ge, fill=0.0, base=0,
                                           pattern=[[0, G], [1, P]], channel_multiplier=-1).then_inc(masked, 1)
                add_types(b, G - 1)

            for c in range(BATCH):
                pool.wait_ge(aggr2_done, 4 * (c + 1))
                pool.tensor_tensor(rstd[:, 4 * c:4 * c + 4], mv[:, 4 * c:4 * c + 4, 1],
                                   eps_c[:].to_broadcast([P, 4]), ALU.add).then_inc(rstd2_step, 1)
                pool.wait_ge(rstd2_step, 2 * c + 1)
                pool.tensor_tensor(rstd[:, 4 * c:4 * c + 4], rstd[:, 4 * c:4 * c + 4],
                                   minus_half[:].to_broadcast([P, 4]), ALU.pow).then_inc(rstd2_step, 1)
            pool.iota(consts_i, pattern=[[1, NC_I]], base=0, channel_multiplier=0).then_inc(route_const, 1)
            pool.iota(tok_i, pattern=[[P, NTILE]], base=0, channel_multiplier=1).then_inc(route_const, 1)
            pool.wait_ge(route_const, 2)
            pool.tensor_scalar(order_e, consts_i[:, 0:EXPERTS], -1.0, float(EXPERTS), ALU.mult, ALU.add).then_inc(row_tail, 1)
            pool.tensor_scalar(steps, consts_i[:, 0:NTILE], float(P), None, ALU.mult).then_inc(row_tail, 1)
            pool.tensor_scalar(tile_no, consts_i[:, 0:RTILES], 1.0, None, ALU.mult).then_inc(row_tail, 1)
            pool.memset(ones_e, 1.0).then_inc(row_tail, 1)
            pool.memset(restart, 1.0).then_inc(row_tail, 1)
            pool.wait_ge(row_tail, 5)
            pool.memset(restart.rearrange("p (e n) -> p e n", e=EXPERTS)[:, :, 0:1], 0.0).then_inc(route_const, 1)

            pool.wait_ge(slots_ready, 1)
            pool.wait_ge(xr_ready, NTILE)
            pool.wait_ge(pad_out, 16)
            pool.tensor_copy(xr[:, :, DM].bitcast(I32), tok_i).then_inc(row_tail, 1)
            for k in range(2):
                pool.wait_ge(slots_ready, k + 1)
                if k:
                    pool.wait_ge(scattered, 16 * NTILE)
                pool.tensor_copy(xr[:, :, DM + 1], wts[:, k]).then_inc(row_tail, 1)
                pool.wait_ge(row_tail, 7 + k)
                for n in range(NTILE):
                    pool.indirect_dma_start(out=routed_rows[:, :], out_offset=bass.IndirectOffsetOnAxis(
                        ap=slot_i[:, k, n:n + 1].bitcast(mybir.dt.uint32), axis=0), in_=xr[:, n, :], in_offset=None).then_inc(scattered, 16)

            pool.wait_ge(row_out, ROW0 + 16 * NTILE)
            pool.wait_ge(dummy_out, 16)

            def add_rows(rt, r):
                pool.wait_ge(yout_ready, YO0 + NTILE + rt + 1)
                alone()
                pool.indirect_dma_start(out=out[:, :], out_offset=bass.IndirectOffsetOnAxis(
                    ap=xrow[:, r, DM:DM + 1].bitcast(mybir.dt.uint32), axis=0), in_=yout[:, r % 2], in_offset=None,
                    compute_op=ALU.add).then_inc(row_added, 16)
                pool.wait_ge(row_added, 16 * (rt + 1))
                pool.sem_inc(add_turn, 1)

            with pool.Fori(0, RTILES // 4) as i:
                for r in range(4):
                    add_rows(4 * i + r, r)
            for rt in range(RTILES // 4 * 4, RTILES):
                add_rows(rt, rt % 4)

        @block.tensor
        def _(pe):
            for s, n in ((tr_done, TR0), (mm_done, MM0), (misc_ready, MR0), (av_done, AV0),
                         (up_done, UP0), (down_done, DOWN0)):
                pe.sem_inc(s, n)
            pe.wait_ge(consts_ready, 11)
            pe.wait_ge(proj_in, 16 * 6)

            def to_columns(b, k):
                pe.wait_ge(trT_ready, TRT0 + 3 * b + k - 2)
                src = xn if k < 2 else ctx_b
                for t in range(QT):
                    mm = pe.transpose(ps[:, TR_BANK[k], P * t:P * t + P], src[:, t, P * (k % 2):P * (k % 2) + P], ident[:])
                mm.then_inc(tr_done, 1)

            SPLITS = [i for i, o in enumerate(OUTPUTS) if o[0] == "split"]
            VALUES = [i for i, o in enumerate(OUTPUTS) if o[0] == "value"]
            with pe.Fori(0, BATCH) as b:
                pe.wait_ge(xn_ready, 4 * b + 4)
                to_columns(b, 0)
                to_columns(b, 1)
                for i, (kind, t, half) in enumerate(OUTPUTS):
                    if i == 4:
                        pe.wait_ge(ctx_staged, b + 1)
                        to_columns(b, 2)
                    if i == 0:
                        pe.wait_ge(trT_ready, TRT0 + 3 * b + 2)
                    if i == 8:
                        pe.wait_ge(trT_ready, TRT0 + 3 * b + 3)
                    before_i, bb = (i - MM_RING, b) if i >= MM_RING else (i - MM_RING + len(OUTPUTS), b - 1)
                    if before_i in SPLITS:
                        pe.wait_ge(split_high, HIGH0 + 2 * (NSPLIT * bb + SPLITS.index(before_i) + 1))
                    else:
                        pe.wait_ge(value_ready, VAL0 + NVALUE * bb + VALUES.index(before_i) + 1)
                    bank = ps[:, MM_BANK + i % MM_RING]
                    if kind == "split" and t < 3:
                        for k in range(KT):
                            mm = pe.matmul(bank, wproj[:, t, k, P * half:P * half + P], xnT[:, k], start=k == 0, stop=k == KT - 1)
                    elif kind == "split":
                        mm = pe.matmul(bank, wcross[:, 0, P * half:P * half + P], ctxT, start=True, stop=True)
                    else:
                        for s in range(2):
                            tok = slice(P * (2 * half + s), P * (2 * half + s) + P)
                            dst = bank[:, DM * s:DM * s + DM]
                            if t == 0:
                                for k in range(KT):
                                    mm = pe.matmul(dst, xnT[:, k, tok], wproj[:, 3, k], start=k == 0, stop=k == KT - 1)
                            else:
                                mm = pe.matmul(dst, ctxT[:, tok], wcross[:, 1], start=True, stop=True)
                    mm.then_inc(mm_done, 1)

            def score_unit(u, b, g, k):
                y, qt, pair, keys = a_unit(k)
                pe.wait_ge(a_maxed, AMAX0 + 16 * u + k - 1)
                slot = A_BANK + 2 * (k % 2)
                for s in range(2):
                    h = 2 * pair + s
                    mm = pe.matmul(ps[:, slot + s, 0:keys], stk[0:ROWS, g, 2 * y, h, P * qt:P * qt + P],
                                   stk[0:ROWS, g, 2 * y + 1, h, 0:keys], start=True, stop=bool(y))
                    if not y:
                        mm = pe.matmul(ps[:, slot + s, keys - P:keys], ident_b[:], causal_b[:], start=False, stop=True)
                mm.then_inc(a_scores, 1)

            def key_scores(b, g, v, heads):
                y, j, q0 = key_tile(v)
                for h in heads:
                    pe.wait_ge(exp_done, EXP0 + 4 * (8 * (G * b + g) + v) + h - 1)
                    pe.matmul(ps[:, B_BANK + h % 2, q0:SEQ], stk[0:STACKED, g, 2 * y + 1, h, P * j:P * j + P],
                              stk[0:STACKED, g, 2 * y, h, q0:SEQ], start=True, stop=True).then_inc(b_scores, 1)

            def times_values(b, g, v):
                y, j, q0 = key_tile(v)
                u = G * b + g
                if v == 0:
                    pe.wait_ge(v_staged, u + 1)
                if j == 0:
                    pe.wait_ge(o_copied, OC0 + 2 * u + (0 if y else 1))
                    if g == 0 and y:
                        pe.wait_ge(x2_ready, X20 + 2 * b)
                pe.wait_ge(exp_done, EXP0 + 4 * (8 * u + v) + 4)
                if not y:
                    pe.wait_ge(masked, 4 * u + j + 1)
                for h in range(G):
                    mm = pe.matmul(ps[32 * h:32 * h + 32, O_BANK, q0:SEQ], vaug[:, g % 2, v, h], prob[:, v % 4, h, q0:SEQ],
                                   start=j == 0, stop=j == QT - 1)
                mm.then_inc(av_done, 1)

            def max_to_rows(u, r, wait_job):
                pe.wait_ge(a_maxed, AMAX0 + 16 * u + 16)
                pe.wait_ge(misc_free, MISC0 + wait_job)
                pe.transpose(ps[0:32, MISC_BANK, 0:P], maxes[:, r].rearrange("p y h q -> p (y h q)"),
                             ident[:]).then_inc(misc_ready, 1)

            def o_to_rows(b, g, y):
                u = G * b + g
                pe.wait_ge(o_copied, OC0 + 2 * u + (1 if y else 2))
                pe.wait_ge(misc_free, MISC0 + job(b, "y", g, y))
                for t in range(QT):
                    mm = pe.transpose(ps[:, MISC_BANK, P * t:P * t + P], osb[:, y, P * t:P * t + P], ident[:])
                mm.then_inc(misc_ready, 1)

            def attention_batch(b, last):
                for g in range(G):
                    ahead_g, ahead_b = (g + 2) % G, b + (g + 2) // G
                    pe.wait_ge(stack_in[g], 64 * (b + 1))
                    pe.wait_ge(max_in[g], 32 * (b + 1))
                    if not (last and g >= 2):
                        pe.wait_ge(stack_in[ahead_g], 64 * (ahead_b + 1))
                    for v in range(8):
                        key_scores(b, g, v, (0, 1))
                        if v > 0:
                            times_values(b, g, v - 1)
                        elif g > 0:
                            times_values(b, g - 1, 7)
                        key_scores(b, g, v, (2, 3))
                        if not (last and g >= 2):
                            score_unit(G * b + g + 2, ahead_b, ahead_g, 2 * v)
                            score_unit(G * b + g + 2, ahead_b, ahead_g, 2 * v + 1)
                        if v == 1 and not (last and g == G - 1):
                            max_to_rows(G * b + g + 1, (g + 1) % 2, job(b, "max", g))
                        if v == 2 and g > 0:
                            o_to_rows(b, g - 1, 0)
                        if v == 6:
                            o_to_rows(b, g, 1)
                times_values(b, G - 1, 7)
                o_to_rows(b, G - 1, 0)
                pe.wait_ge(y_added, YA0 + G * b + G)
                pe.wait_ge(misc_free, MISC0 + job(b, "yt"))
                pe.wait_ge(o_copied, OC0 + 2 * (G * b + G))
                for k, bank in enumerate((MISC_BANK, O_BANK)):
                    for t in range(QT):
                        mm = pe.transpose(ps[:, bank, P * t:P * t + P], Y[:, t, P * k:P * k + P], ident[:])
                mm.then_inc(misc_ready, 1)
                pe.wait_ge(yT_ready, b + 1)
                pe.wait_ge(misc_free, MISC0 + job(b, "z"))
                for t in range(QT):
                    bank = (MISC_BANK, O_BANK)[t // 2]
                    for k in range(KT):
                        mm = pe.matmul(ps[:, bank, DM * (t % 2):DM * (t % 2) + DM], YT[:, k, P * t:P * t + P], wp_sb[:, k],
                                       start=k == 0, stop=k == KT - 1)
                mm.then_inc(misc_ready, 1)

            pe.wait_ge(ones_rows, 1)
            for u in range(2):
                pe.wait_ge(stack_in[u], 64)
                for k in range(16):
                    score_unit(u, 0, u, k)
                if u == 0:
                    max_to_rows(0, 0, 0)
            with pe.Fori(0, BATCH - 1) as b:
                attention_batch(b, False)
            attention_batch(BATCH - 1, True)

            pe.wait_ge(x2_ready, X20 + 2 * BATCH)
            for n in range(NTILE + 1):
                if n < NTILE:
                    pe.wait_ge(xr_ready, n + 1)
                    if n >= 2:
                        pe.wait_ge(x2nT_ready, n - 1)
                    for k in range(KT):
                        mm = pe.transpose(ps[:, n % 2, P * k:P * k + P], xr[:, n, P * k:P * k + P], ident[:])
                    mm.then_inc(t2_done, 1)
                if n >= 1:
                    m = n - 1
                    pe.wait_ge(x2nT_ready, m + 1)
                    for k in range(KT):
                        mm = pe.matmul(ps[:, 2, EXPERTS * m:EXPERTS * m + EXPERTS], x2nT[:, m % 2, k], wg_sb[:, k],
                                       start=k == 0, stop=k == KT - 1)
                    mm.then_inc(logits_done, 1)

            def rows_to_columns(t, r, turn):
                pe.wait_ge(row_in[r], 16 * turn)
                pe.wait_ge(xT_ready, XT0 + t)
                for k in range(KT):
                    mm = pe.transpose(ps[:, 0, P * k:P * k + P], xrow[:, r, P * k:P * k + P], ident[:])
                mm.then_inc(xt_done, 1)

            def up(t, r, e):
                pe.wait_ge(xT_ready, XT0 + t + 1)
                pe.wait_ge(hid_ready, HID0 + t - 1)
                for m in range(2):
                    for k in range(KT):
                        mm = pe.matmul(ps[:, 1 + 2 * m + r % 2], xT[:, r % 2, k], w13[:, e, m, k], start=k == 0, stop=k == KT - 1)
                mm.then_inc(up_done, 1)

            def down(t, r, e):
                pe.wait_ge(hid_ready, HID0 + t + 1)
                pe.wait_ge(hT_ready, HT0 + t)
                for f in range(FT):
                    mm = pe.transpose(ps[:, 5, P * f:P * f + P], hid[:, r % 2, P * f:P * f + P], ident[:])
                mm.then_inc(ht_done, 1)
                pe.wait_ge(hT_ready, HT0 + t + 1)
                pe.wait_ge(yout_ready, YO0 + t - 1)
                for f in range(FT):
                    mm = pe.matmul(ps[:, 6 + r % 2, 0:DM], hT[:, r % 2, f], w2[:, e, f], start=f == 0, stop=f == FT - 1)
                mm.then_inc(down_done, 1)

            pe.wait_ge(shared_w_in, 16 * 3)
            rows_to_columns(0, 0, 1)
            rows_to_columns(1, 1, 1)
            pe.wait_ge(expz_ready, 1)
            up(0, 0, EXPERTS)
            pe.wait_ge(chosen_ready, 1)
            flat = chosen_b.rearrange("p e n -> p (e n)")
            pe.matmul(ps[:, 7, 0:NE], before_b[:], flat, start=True, stop=True)
            pe.matmul(ps[:, 7, NE:2 * NE], ones_b[:], flat, start=True, stop=True).then_inc(counts_done, 1)

            with pe.Fori(0, NTILE // 4 - 1) as i:
                for r in range(4):
                    t = 4 * i + r
                    rows_to_columns(t + 2, (r + 2) % 4, i + 1 + (r + 2) // 4)
                    up(t + 1, r + 1, EXPERTS)
                    down(t, r, EXPERTS)
            for t in range(NTILE - 4, NTILE):
                rows_to_columns(t + 2, (t + 2) % 4, (t + 2) // 4 + 1)
                if t + 1 < NTILE:
                    up(t + 1, t + 1, EXPERTS)
                else:
                    pe.wait_ge(emap_ready, 1)
                    pe.wait_ge(expert_w_in, 16 * 3 * EXPERTS)
                    first = pe.value_load(emap[0:1, 0:1], min_val=0, max_val=EXPERTS - 1)
                    up(t + 1, t + 1, first)
                down(t, t, EXPERTS)
            turns = NTILE // 4

            def expert(rt):
                return pe.value_load(emap[0:1, bass.ds(rt, 1)], min_val=0, max_val=EXPERTS - 1)

            with pe.Fori(0, (RTILES - 2) // 4) as i:
                for r in range(4):
                    rt = 4 * i + r
                    rows_to_columns(NTILE + rt + 2, (r + 2) % 4, turns + i + 1 + (r + 2) // 4)
                    up(NTILE + rt + 1, r + 1, expert(rt + 1))
                    down(NTILE + rt, r, expert(rt))
            for rt in range((RTILES - 2) // 4 * 4, RTILES):
                if rt + 2 < RTILES:
                    rows_to_columns(NTILE + rt + 2, (rt + 2) % 4, turns + (rt + 2) // 4 + 1)
                if rt + 1 < RTILES:
                    up(NTILE + rt + 1, rt + 1, expert(rt + 1))
                down(NTILE + rt, rt, expert(rt))


_INS = ["x", "ctx_512", "g_xattn", "g_ffn", "L0_xattn_Wk", "L0_xattn_bk", "L0_xattn_Wq", "L0_xattn_bq", "L0_xattn_Wv",
        "L0_xattn_bv", "L0_xattn_Wck", "L0_xattn_bck", "L0_xattn_Wcq", "L0_xattn_bcq", "L0_xattn_Wcv", "L0_xattn_bcv",
        "L0_xattn_Wp", "L0_xattn_bp", "L0_ffn_Wg", "L0_ffn_Ws1", "L0_ffn_Ws3", "L0_ffn_Ws2", "L0_ffn_We1", "L0_ffn_We3",
        "L0_ffn_We2"]


def kernel(**inputs):
    import numpy as np
    import concourse.bacc as bacc
    from concourse.bass_utils import run_bass_kernel_spmd

    nc = bacc.Bacc("TRN2", target_bir_lowering=False, num_devices=1)
    arrays, args = {}, []
    for name in _INS:
        a = np.ascontiguousarray(inputs[name])
        if name in ("x", "ctx_512"):
            a = a.reshape(TOK, a.shape[-1])
        arrays[f"in_{name}"] = a
        args.append(nc.dram_tensor(f"in_{name}", a.shape, mybir.dt.from_np(a.dtype), kind="ExternalInput").ap())
    args.append(nc.dram_tensor("out_0", (TOK + P, DM), F32, kind="ExternalOutput").ap())
    build(nc, *args)
    r = run_bass_kernel_spmd(nc, [arrays], core_ids=[0])
    return r.results[0]["out_0"][:TOK].reshape(BATCH, SEQ, DM)
```

```python
from contextlib import ExitStack

import concourse.bass as bass
import numpy as np
from concourse import mybir

F32 = mybir.dt.float32
BF16 = mybir.dt.bfloat16
I32 = mybir.dt.int32
ALU = mybir.AluOpType
ACT = mybir.ActivationFunctionType
AX = mybir.AxisListType.X

P = 128
BATCH, SEQ, DM, DC = 4, 512, 256, 128
HEADS, HD = 16, 16
EXPERTS, FF, TOPK = 8, 512, 2
KT = DM // P
QT = SEQ // P
TOK = BATCH * SEQ
NTILE = TOK // P
G = 4
SLOTS = 6
ROWS = HD * SLOTS
STACKED = ROWS + 2
SCALE = float(HD) ** -0.5
EPS = 1e-5
NEG = -1e30
RTILES = (TOK * TOPK + EXPERTS * (P - 1)) // P
XW = DM + 2
FT = FF // P
TR_BANK = (0, 1, 2)
MM_BANK, MM_RING = 4, 4
A_BANK = 0
B_BANK = 4
O_BANK, MISC_BANK = 6, 7
DOWN_BANK = 6

OUTPUTS = [("split", 0, 0), ("split", 0, 1), ("split", 1, 0), ("split", 1, 1), ("value", 0, 0), ("value", 0, 1),
           ("split", 2, 0), ("split", 2, 1), ("split", 3, 0), ("split", 3, 1), ("value", 1, 0), ("value", 1, 1)]
NSPLIT = sum(o[0] == "split" for o in OUTPUTS)
NVALUE = len(OUTPUTS) - NSPLIT
SPLIT_RING = 4
ACT_MIDS = (1, 3, 5, 7)


def build(nc, x, ctx_in, w_proj, w_cross, w_out, part_bias, row_params, Wg, Ws1, Ws3, Ws2, We1, We3, We2, out):
    with ExitStack() as ctx:
        def sb(name, shape, dt=F32):
            return ctx.enter_context(nc.sbuf_tensor(name, shape, dt))

        def sem(name):
            return ctx.enter_context(nc.semaphore(name))

        stacks = nc.dram_tensor("stacks", [BATCH, 4, 3, HD, HEADS, SEQ], BF16).ap()
        maxrows = nc.dram_tensor("maxrows", [BATCH * G, 2, G * QT, 2, P], BF16).ap()
        shared_rows = nc.dram_tensor("shared_rows", [TOK, DM], F32).ap()
        routed_rows = nc.dram_tensor("routed_rows", [RTILES * P, XW], F32).ap()

        ps = ctx.enter_context(nc.psum_tensor("ps", [P, 8, 512], F32))

        ident = sb("ident", [P, P])
        ident_b = sb("ident_b", [P, P], BF16)
        causal = sb("causal", [P, P])
        causal_b = sb("causal_b", [P, P], BF16)
        before = sb("before", [P, P])
        before_b = sb("before_b", [P, P], BF16)
        ones_b = sb("ones_b", [P, P], BF16)
        eps_c = sb("eps_c", [P, 1])
        minus_half = sb("minus_half", [P, 1])

        bias = sb("bias", [P, 4, 2])
        row_sb = sb("row_sb", [P, 3 * DM + 2])
        rowb = row_sb[:, 0:3 * DM].rearrange("p (t c) -> p t c", t=3)
        gates_g = row_sb[:, 3 * DM:3 * DM + 2]
        tanh_g = sb("tanh_g", [P, 2])
        ffn_c = sb("ffn_c", [P, 1])
        tbp = sb("tbp", [P, DM])

        xall = sb("xall", [P, NTILE, DM])
        V = sb("V", [P, BATCH, 2, QT, DM])

        NW = EXPERTS + 1
        w_words = NW * (2 * KT * FF + FT * DM)
        arena = sb("arena", [P, w_words])
        at = [0]

        def cut(words):
            at[0] += words
            assert at[0] <= w_words
            return arena[:, at[0] - words:at[0]]

        stk = cut(G * 4 * G * SEQ // 2).bitcast(BF16).rearrange("p (s t h q) -> p s t h q", s=G, t=4, h=G)
        ONE_PAIR = float(np.uint32(0x3F803F80).view(np.float32))
        stk_pairs = arena[ROWS:STACKED, 0:G * 4 * G * SEQ // 2].rearrange("p (s y t w) -> p s y t w", s=G, y=2, t=2)

        def key_ones(half):
            return stk_pairs[:, 2 * half:2 * half + 2, :, 1].rearrange("p s y w -> p (s y) w")

        prob_words = cut(4 * G * SEQ)
        prob = prob_words.rearrange("p (s h q) -> p s h q", s=4, h=G)
        assert at[0] <= EXPERTS * w_words // NW
        w_e = arena[:].rearrange("p (e w) -> p e w", e=NW)
        w13 = w_e[:, :, 0:2 * KT * FF].rearrange("p e (m k f) -> p e m k f", m=2, k=KT)
        w2 = w_e[:, :, 2 * KT * FF:].rearrange("p e (f n) -> p e f n", f=FT)

        s2_words = 9768
        arena2 = sb("arena2", [P, s2_words])
        at2 = [0]

        def cut2(words):
            at2[0] += words
            assert at2[0] <= s2_words, at2[0]
            return arena2[:, at2[0] - words:at2[0]]

        wproj = prob_words[:, 0:4 * KT * DM].rearrange("p (w k n) -> p w k n", w=4, k=KT)
        wcross = prob_words[:, 4 * KT * DM:4 * KT * DM + 2 * DM].rearrange("p (w n) -> p w n", w=2)
        ctx_sb = prob_words[:, 4 * KT * DM + 2 * DM:4 * KT * DM + 2 * DM + NTILE * DC].rearrange(
            "p (n c) -> p n c", n=NTILE)
        wp_sb = sb("wp_sb", [P, KT, DM])
        stats = sb("stats", [P, NTILE, 6])
        mv = sb("mv", [P, NTILE, 2])
        rstd = sb("rstd", [P, NTILE])
        xn = cut2(4 * DM).rearrange("p (t c) -> p t c", t=4)
        xnT = cut2(KT * SEQ).rearrange("p (k t) -> p k t", k=KT)
        ctxT = cut2(SEQ)
        q32 = cut2(2 * SEQ).rearrange("p (r t) -> p r t", r=2)
        rest = cut2(2 * SEQ).rearrange("p (r t) -> p r t", r=2)
        parts = cut2(SPLIT_RING * 3 * SEQ // 2).bitcast(BF16).rearrange("p (r s t) -> p r s t", r=SPLIT_RING, s=3)
        ctx_b = cut2(SEQ).rearrange("p (t c) -> p t c", t=QT)
        at2[0] = 0
        vaug_words = cut2(2 * 8 * G * 32)
        vaug = vaug_words.rearrange("p (r v h c) -> p r v h c", r=2, v=8, h=G)
        osb = cut2(2 * SEQ).rearrange("p (y q) -> p y q", y=2)
        ynorm = cut2(2 * QT * G * HD).rearrange("p (y q h d) -> p y q h d", y=2, q=QT, h=G)
        Y = cut2(QT * DM).rearrange("p (t c) -> p t c", t=QT)
        YT = cut2(KT * SEQ).rearrange("p (k t) -> p k t", k=KT)
        recip = cut2(2 * QT * G).rearrange("p (y q h) -> p y q h", y=2, q=QT)
        th = vaug_words[:, 0:2 * FF].rearrange("p (r f) -> p r f", r=2)
        gated = vaug_words[:, 2 * FF:4 * FF].rearrange("p (r f) -> p r f", r=2)
        xrow = cut2(4 * XW).rearrange("p (r c) -> p r c", r=4)
        xT = cut2(2 * KT * P).rearrange("p (r k t) -> p r k t", r=2, k=KT)
        hid = cut2(2 * FF).rearrange("p (r f) -> p r f", r=2)
        xstage = hid.rearrange("p r f -> p (r f)").rearrange("p (t c) -> p t c", t=QT)
        hT = cut2(2 * FF).rearrange("p (r f t) -> p r f t", r=2, f=FT)
        yout = cut2(2 * DM).rearrange("p (r c) -> p r c", r=2)
        wg_sb = sb("wg_sb", [P, KT, EXPERTS])
        xr = V[:, :, :, :, :].rearrange("p b y q c -> p (b y q c)")[:, 0:NTILE * XW].rearrange(
            "p (n c) -> p n c", n=NTILE)
        rt = V[:, :, :, :, :].rearrange("p b y q c -> p (b y q c)")[:, NTILE * XW:]
        rat = [0]

        def rcut(words):
            rat[0] += words
            assert rat[0] <= BATCH * 2 * QT * DM - NTILE * XW
            return rt[:, rat[0] - words:rat[0]]

        NE = NTILE * EXPERTS

        def rcut3():
            return rcut(NE).rearrange("p (n e) -> p n e", n=NTILE)

        expz = sb("expz", [P, NTILE, EXPERTS])
        gate, top1, top2, pick = (rcut3() for _ in range(4))
        slot_e = rcut(NE).rearrange("p (e n) -> p e n", e=EXPERTS)
        chosen_b = rcut(NE // 2).bitcast(BF16).rearrange("p (e n) -> p e n", e=EXPERTS)
        best = rcut(NTILE * 8).rearrange("p (n e) -> p n e", n=NTILE)
        order_e = rcut(EXPERTS)
        rankv = rcut3()
        firstm = rcut3()
        gsum, ginv = rcut(NTILE), rcut(NTILE)
        wts = rcut(2 * NTILE).rearrange("p (k n) -> p k n", k=2)
        slot_f = rcut(2 * NTILE).rearrange("p (k n) -> p k n", k=2)
        slot_i = rcut(2 * NTILE).bitcast(I32).rearrange("p (k n) -> p k n", k=2)
        tok_i = rcut(NTILE).bitcast(I32)
        restart = rcut(NE)
        run_tot, slot_en = rcut(NE), rcut(NE)
        ones_e, starts = rcut(EXPERTS), rcut(EXPERTS)
        NC_I = max(RTILES, NTILE, EXPERTS)
        consts_i = rcut(NC_I).bitcast(I32)
        steps = rcut(NTILE)
        over = rcut(NE).rearrange("p (e n) -> p e n", e=EXPERTS)
        ntiles = rcut(EXPERTS)
        ends = rcut(EXPERTS)
        tile_no = rcut(RTILES)
        passed = rcut(RTILES * EXPERTS).rearrange("p (t e) -> p t e", t=RTILES)
        emap_f = rcut(RTILES)
        emap = rcut(RTILES).bitcast(I32)
        pad = sb("pad", [P, XW])
        maxes = sb("maxes", [P, 2, 2, G, QT])
        mrow = sb("mrow", [2 * QT * G, 2, 2, P], BF16)

        def ahead(name, n):
            return sem(name), n

        consts_ready, bias_in, row_params_in, late_in, ctx_loaded = (
            sem(n) for n in ("consts_ready", "bias_in", "row_params_in", "late_in", "ctx_loaded"))
        proj_in = [sem(f"proj_in{t}") for t in range(5)]
        x_in = [sem(f"x_in{b}") for b in range(BATCH)]
        shared_w_in, expert_w_in = sem("shared_w_in"), sem("expert_w_in")
        tanh_ready, tbp_ready, ffn_c_ready = sem("tanh_ready"), sem("tbp_ready"), sem("ffn_c_ready")
        stats_done, aggr_done, rstd_step, xn_ready = sem("stats_done"), sem("aggr_done"), sem("rstd_step"), sem("xn_ready")
        tr_done, TR0 = ahead("tr_done", 1)
        trT_ready, TRT0 = ahead("trT_ready", 3)
        mm_done, MM0 = ahead("mm_done", 1)
        split_high, HIGH0 = ahead("split_high", 4)
        split_rest, REST0 = ahead("split_rest", 2)
        split_mid = sem("split_mid")
        split_mid_act = sem("split_mid_act")
        split_low, LOW0 = ahead("split_low", 2)
        value_ready, VAL0 = ahead("value_ready", 2)
        parts_out = [sem(f"parts_out{r}") for r in range(SPLIT_RING)]
        PARTS0 = 16
        rstd_const, ctx_staged, ones_rows, vaug_clear = sem("rstd_const"), sem("ctx_staged"), sem("ones_rows"), sem("vaug_clear")
        STACK_DMAS = 16 * 4 * 3
        stack_in = [sem(f"stack_in{g}") for g in range(G)]
        max_in = [sem(f"max_in{g}") for g in range(G)]
        a_scores = sem("a_scores")
        a_maxed, AMAX0 = ahead("a_maxed", 2)
        misc_ready, MR0 = ahead("misc_ready", 16)
        misc_free, MISC0 = ahead("misc_free", 1)
        mrow_high, mrow_ready = sem("mrow_high"), sem("mrow_ready")
        mrow_out = sem("mrow_out")
        MROW0 = 16
        v_staged = sem("v_staged")
        b_scores = sem("b_scores")
        exp_done, EXP0 = ahead("exp_done", 2)
        masked = sem("masked")
        av_done, AV0 = ahead("av_done", 16)
        o_copied, OC0 = ahead("o_copied", 1)
        recip_done = sem("recip_done")
        ynorm_ready = sem("ynorm_ready")
        y_added, YA0 = ahead("y_added", 1)
        xb_ready = sem("xb_ready")
        stats2_done, aggr2_done, rstd2_step, xr_ready = (sem(n) for n in ("stats2_done", "aggr2_done", "rstd2_step", "xr_ready"))
        xr_kept = sem("xr_kept")
        shared_in = sem("shared_in")
        pad_ready, pad_out, dummy_out = sem("pad_ready"), sem("pad_out"), sem("dummy_out")
        route_const, route_step, chosen_ready, counts_done = (
            sem(n) for n in ("route_const", "route_step", "chosen_ready", "counts_done"))
        emap_ready, slots_ready, row_tail = sem("emap_ready"), sem("slots_ready"), sem("row_tail")
        scattered = sem("scattered")
        row_in = [sem(f"row_in{r}") for r in range(4)]
        xt_done = sem("xt_done")
        xT_ready, XT0 = ahead("xT_ready", 1)
        up_done, UP0 = ahead("up_done", 4)
        tanh_done = sem("tanh_done")
        gated_ready = sem("gated_ready")
        hid_ready, HID0 = ahead("hid_ready", 2)
        ht_done = sem("ht_done")
        hT_ready, HT0 = ahead("hT_ready", 1)
        down_done, DOWN0 = ahead("down_done", 2)
        yout_ready, YO0 = ahead("yout_ready", 2)
        row_out = [sem(f"row_out{r}") for r in range(2)]
        ROWS_OUT = 16 * NTILE // 2
        pool_waited = sem("pool_waited")
        dve_waited = sem("dve_waited")
        row_added = sem("row_added")
        add_turn, ADD0 = ahead("add_turn", 2)

        assert RTILES % (BATCH - 1) == 0
        PAD_TILES = RTILES // (BATCH - 1)
        routed_tiles = routed_rows.rearrange("(t p) c -> p t c", p=P)
        x_tiles = x.rearrange("(n p) c -> p n c", p=P)
        ctx_tiles = ctx_in.rearrange("(n p) c -> p n c", p=P)
        out_tiles = out.rearrange("(n p) c -> n p c", p=P)

        block = ctx.enter_context(nc.Block())

        def key_tile(v):
            y, j = (1, v) if v < QT else (0, v - QT)
            return y, j, (0 if y else P * j)

        def b_bank(b, g, h):
            if isinstance(b, int) and b == BATCH - 1 and g >= 2:
                return (B_BANK + h if h < 2 else A_BANK + h - 2), 4
            return B_BANK + h % 2, 2

        def a_unit(k):
            y, r = (1, k) if k < 8 else (0, k - 8)
            qt, pair = r // 2, r % 2
            return y, qt, pair, (SEQ if y else P * (qt + 1))

        JOBS = [("max", 0), ("prev", "y"), ("prev", "yt0"), ("prev", "yt1"), ("prev", "z0"), ("y", 0, 1), ("prev", "z1"),
                ("max", 1), ("y", 0, 0), ("y", 1, 1),
                ("max", 2), ("y", 1, 0), ("prev", "rt0"), ("prev", "rt1"), ("prev", "logits"), ("y", 2, 1),
                ("max", 3), ("y", 2, 0), ("y", 3, 1)]
        PREV_JOBS = [j for j in JOBS if j[0] == "prev"]

        def job(b, *what):
            if isinstance(b, int) and b == BATCH:
                return len(JOBS) * BATCH - len(PREV_JOBS) + PREV_JOBS.index(what)
            n = JOBS.index(what)
            if isinstance(b, int) and b == 0:
                return 1 + [j for j in JOBS if j not in PREV_JOBS].index(what)
            if isinstance(b, int) and b == BATCH - 1 and n > JOBS.index(("max", G - 1)):
                n -= 1
            return len(JOBS) * b + n + 1 - len(PREV_JOBS)

        @block.sync
        def _(sp):
            for b in range(BATCH):
                sp.dma_start(xall[:, 4 * b:4 * b + 4, :], x_tiles[:, 4 * b:4 * b + 4, :]).then_inc(x_in[b], 16)
                if b == 0:
                    sp.dma_start(ctx_sb, ctx_tiles).then_inc(ctx_loaded, 16)
            for r in range(SPLIT_RING):
                sp.sem_inc(parts_out[r], PARTS0)
            sp.sem_inc(mrow_out, MROW0)
            per_batch = 16 * (NSPLIT // SPLIT_RING)

            def load_stack(b, g):
                for t in range(4):
                    at_slot = 0
                    for run in (((0, 0, 0), (1, 1), (2,)) if t % 2 == 0 else ((0, 1, 2), (0, 1), (0,))):
                        dst = stk[HD * at_slot:HD * (at_slot + len(run)), g, t]
                        if len(set(run)) == 1:
                            src = stacks[b, t, run[0], :, G * g:G * g + G].rearrange("d h q -> d (h q)").unsqueeze(
                                0).to_broadcast([len(run), HD, G * SEQ])
                        else:
                            src = stacks[b, t, run[0]:run[-1] + 1, :, G * g:G * g + G].rearrange("s d h q -> (s d) (h q)")
                        sp.dma_start(dst.rearrange("p h q -> p (h q)"), src).then_inc(stack_in[g], 16)
                        at_slot += len(run)

            for b in range(BATCH):
                for n in range(NSPLIT):
                    t, half, r = n // 2, n % 2, n % SPLIT_RING
                    sp.wait_ge(split_low, LOW0 + NSPLIT * b + n + 1)
                    sp.dma_start(stacks[b, t].rearrange("s (m d) h q -> m (d h) s q", m=2)[half],
                                 parts[:, r]).then_inc(parts_out[r], 16)
                    if b and n == SPLIT_RING:
                        for rr in range(SPLIT_RING):
                            sp.wait_ge(parts_out[rr], PARTS0 + per_batch)
                        load_stack(0, b - 1)
            load_stack(0, G - 1)
            sp.dma_start(w13[:, EXPERTS, 0], Ws1.rearrange("(k p) f -> p k f", p=P)).then_inc(shared_w_in, 16)
            sp.dma_start(w13[:, EXPERTS, 1], Ws3.rearrange("(k p) f -> p k f", p=P)).then_inc(shared_w_in, 16)
            sp.dma_start(w2[:, EXPERTS], Ws2.rearrange("(k p) n -> p k n", p=P)).then_inc(shared_w_in, 16)
            sp.wait_ge(pad_ready, 1)

            def max_rows(u, r, g):
                sp.wait_ge(mrow_ready, u + 1)
                sp.dma_start(maxrows[u].rearrange("y c s q -> (y c) s q"), mrow[:, r]).then_inc(mrow_out, 16)
                sp.wait_ge(mrow_out, MROW0 + 16 * (u + 1))
                for y in range(2):
                    sp.dma_start(stk[ROWS:STACKED, g, 2 * y].rearrange("o h (t q) -> o (h t) q", t=QT),
                                 maxrows[u, y].rearrange("c s q -> s c q")).then_inc(max_in[g], 16)

            sp.wait_ge(pad_ready, 1)
            max_rows(0, 0, 0)
            for r in range(SPLIT_RING):
                sp.wait_ge(parts_out[r], PARTS0 + BATCH * per_batch)
            with sp.Fori(0, BATCH - 1) as b:
                for g in range(G):
                    max_rows(G * b + g + 1, (g + 1) % 2, (g + 1) % G)
                    sp.wait_ge(av_done, AV0 + 8 * (G * b + g) + 8)
                    load_stack(b + 1, g)
                    if g == 1:
                        sp.dma_start(routed_tiles[:, bass.ds(PAD_TILES * b, PAD_TILES)],
                                     pad[:].unsqueeze(1).to_broadcast([P, PAD_TILES, XW])).then_inc(pad_out, 16)
            sp.dma_start(out[TOK:TOK + P, :], pad[:, 0:DM]).then_inc(dummy_out, 16)
            for g in range(G - 1):
                max_rows(G * (BATCH - 1) + g + 1, (g + 1) % 2, (g + 1) % G)

            sh = shared_rows.rearrange("(n p) c -> n p c", p=P)
            ro = routed_rows.rearrange("(n p) c -> n p c", p=P)
            sp.wait_ge(shared_in, 16)
            for t in range(4):
                sp.dma_start(xrow[:, t, 0:DM], sh[t]).then_inc(row_in[t], 16)
            sp.wait_ge(av_done, AV0 + 8 * G * BATCH)
            for t in range(NTILE):
                r = t % 4
                sp.wait_ge(yout_ready, YO0 + t + 1)
                sp.dma_start(out_tiles[t], yout[:, r % 2]).then_inc(row_out[r % 2], 16)
                if t + 4 < NTILE:
                    sp.wait_ge(shared_in, 16 * ((t + 4) // QT + 1))
                    sp.dma_start(xrow[:, r, 0:DM], sh[t + 4]).then_inc(row_in[r], 16)
                else:
                    if r == 0:
                        sp.wait_ge(scattered, 16 * 2 * NTILE)
                    sp.dma_start(xrow[:, r], ro[r]).then_inc(row_in[r], 16)
                if t < EXPERTS:
                    sp.dma_start(w13[:, t, 0], We1[t].rearrange("(k p) f -> p k f", p=P)).then_inc(expert_w_in, 16)
                    sp.dma_start(w13[:, t, 1], We3[t].rearrange("(k p) f -> p k f", p=P)).then_inc(expert_w_in, 16)
                    sp.dma_start(w2[:, t], We2[t].rearrange("(k p) n -> p k n", p=P)).then_inc(expert_w_in, 16)
            with sp.Fori(0, (RTILES - 4) // 4) as i:
                for r in range(4):
                    sp.wait_ge(add_turn, ADD0 + 4 * i + r + 1)
                    sp.dma_start(xrow[:, r], ro[4 * i + r + 4]).then_inc(row_in[r], 16)
            for t in range((RTILES - 4) // 4 * 4 + 4, RTILES):
                sp.wait_ge(add_turn, ADD0 + t - 4 + 1)
                sp.dma_start(xrow[:, t % 4], ro[t]).then_inc(row_in[t % 4], 16)
            for r in range(2):
                sp.wait_ge(row_out[r], ROWS_OUT)
            sp.wait_ge(dummy_out, 16)
            sp.wait_ge(row_added, 16 * RTILES)

        @block.scalar
        def _(act):
            for t in range(4):
                act.dma_start(wproj[:, t], w_proj[:, t]).then_inc(proj_in[t], 16)
                if t == 0:
                    act.dma_start(bias[:], part_bias).then_inc(bias_in, 16)
                if t == 1:
                    act.dma_start(row_sb[:], row_params.partition_broadcast(P)).then_inc(row_params_in, 16)
            act.dma_start(wcross, w_cross).then_inc(proj_in[4], 16)
            act.dma_start(wp_sb[:], w_out).then_inc(late_in, 16)
            act.dma_start(wg_sb[:], Wg.rearrange("(k p) n -> p k n", p=P)).then_inc(late_in, 16)
            for s, n in ((trT_ready, TRT0), (split_high, HIGH0), (exp_done, EXP0), (o_copied, OC0), (xT_ready, XT0),
                         (hT_ready, HT0)):
                act.sem_inc(s, n)
            act.wait_ge(bias_in, 16)

            def copy_transposes(b, k):
                act.wait_ge(tr_done, TR0 + 3 * b + k + 1)
                dst = xnT[:, k] if k < 2 else ctxT
                act.copy(dst, ps[:, TR_BANK[k]]).then_inc(trT_ready, 1)

            def projections_batch(b, last):
                n = 0
                for i, (kind, t, half) in enumerate(OUTPUTS):
                    if i == 5:
                        act.wait_ge(mm_done, MM0 + len(OUTPUTS) * b)
                        copy_transposes(b, 2)
                    if i == 8 and not last:
                        act.wait_ge(mm_done, MM0 + len(OUTPUTS) * b + 8)
                        copy_transposes(b + 1, 0)
                        copy_transposes(b + 1, 1)
                    if kind == "value":
                        continue
                    r = n % SPLIT_RING
                    bank = ps[:, MM_BANK + i % MM_RING]
                    act.wait_ge(mm_done, MM0 + len(OUTPUTS) * b + i + 1)
                    act.wait_ge(split_rest, REST0 + NSPLIT * b + n - 1)
                    act.activation(q32[:, n % 2], bank, ACT.Identity,
                                   bias=bias[:, t, half:half + 1]).then_inc(split_high, 1)
                    act.wait_ge(parts_out[r], PARTS0 + 16 * (NSPLIT // SPLIT_RING * b + n // SPLIT_RING))
                    act.activation(parts[:, r, 0], bank, ACT.Identity,
                                   bias=bias[:, t, half:half + 1]).then_inc(split_high, 1)
                    for m in ACT_MIDS:
                        if n == min(m + 1, NSPLIT - 1):
                            act.wait_ge(split_rest, REST0 + NSPLIT * b + m + 1)
                            act.copy(parts[:, m % SPLIT_RING, 1], rest[:, m % 2]).then_inc(split_mid_act, 1)
                    n += 1

            copy_transposes(0, 0)
            copy_transposes(0, 1)
            with act.Fori(0, BATCH - 1) as b:
                projections_batch(b, False)
            projections_batch(BATCH - 1, True)
            act.wait_ge(row_params_in, 16)
            act.activation(tanh_g[:], gates_g, ACT.Tanh).then_inc(tanh_ready, 1)

            def high_rows(b, u, r, *what):
                act.wait_ge(misc_ready, MR0 + (job(b, *what) if what else 0) + 1)
                if what:
                    act.wait_ge(mrow_out, MROW0 + 16 * (u - 1))
                act.activation(mrow[:, r, 0], ps[0:32, MISC_BANK, 0:P], ACT.Copy, scale=-1.0).then_inc(mrow_high, 1)

            def exponentials(b, g, v, before_last=None):
                y, j, q0 = key_tile(v)
                step = 8 * (G * b + g) + v
                act.wait_ge(av_done, AV0 + step - 3)
                for h in range(G):
                    if h == G - 1 and before_last:
                        before_last()
                    act.wait_ge(b_scores, 4 * step + h + 1)
                    act.activation(prob[:, v % 4, h, q0:SEQ], ps[:, b_bank(b, g, h)[0], q0:SEQ], ACT.Exp,
                                   scale=SCALE).then_inc(exp_done, 1)

            def copy_o(b, g, y):
                u = G * b + g
                act.wait_ge(av_done, AV0 + 8 * u + (4 if y else 8))
                if g:
                    act.wait_ge(misc_ready, MR0 + job(b, "y", g - 1, y) + 1)
                elif not (isinstance(b, int) and b == 0):
                    act.wait_ge(misc_ready, MR0 + (job(b - 1, "y", G - 1, 1) if y else job(b, "prev", "y")) + 1)
                act.copy(osb[:, y], ps[:, O_BANK]).then_inc(o_copied, 1)

            def columns_out(b, name):
                act.wait_ge(misc_ready, MR0 + job(b, "prev", name) + 1)
                act.copy(YT[:, int(name[-1])], ps[:, MISC_BANK]).then_inc(misc_free, 1)

            def router_exp(b):
                act.wait_ge(misc_ready, MR0 + job(b, "prev", "logits") + 1)
                act.activation(expz[:, bass.ds(QT * (b - 1), QT)].rearrange("p n e -> p (n e)"),
                               ps[:, MISC_BANK, 0:QT * EXPERTS], ACT.Exp, scale=-1.0).then_inc(misc_free, 1)

            def store_rows(b):
                act.wait_ge(xr_ready, QT * b)
                act.dma_start(shared_rows.rearrange("(n p) c -> p n c", p=P)[:, bass.ds(QT * (b - 1), QT)],
                              xr[:, NTILE - QT:NTILE, 0:DM] if b is BATCH else xstage).then_inc(shared_in, 16)

            def attention_batch(b, first, last):
                for g in range(G):
                    for v in range(8):
                        if v == 1 and g > 0:
                            exponentials(b, g, v, lambda: copy_o(b, g - 1, 0))
                        elif v == 1 and not first:
                            exponentials(b, g, v, lambda: copy_o(b - 1, G - 1, 0))
                        elif v == 5:
                            exponentials(b, g, v, lambda: copy_o(b, g, 1))
                        else:
                            exponentials(b, g, v)
                        if v == 1 and not (last and g == G - 1):
                            high_rows(b, G * b + g + 1, (g + 1) % 2, "max", g)
                        if not first and v in (3, 4) and g in (0, 2):
                            columns_out(b, ("yt" if g == 0 else "rt") + str(v - 3))
                        if not first and (g, v) == (2, 5):
                            router_exp(b)
                        if not first and (g, v) == (2, 3):
                            store_rows(b)

            high_rows(0, 0, 0)
            attention_batch(0, True, False)
            with act.Fori(1, BATCH - 1) as b:
                attention_batch(b, False, False)
            attention_batch(BATCH - 1, False, True)
            copy_o(BATCH - 1, G - 1, 0)

            def copy_rows(t, r):
                act.wait_ge(xt_done, t + 1)
                act.wait_ge(up_done, UP0 + 2 * t - 2)
                act.copy(xT[:, r % 2].rearrange("p k t -> p (k t)"), ps[:, 0, 0:DM]).then_inc(xT_ready, 1)

            def tanh(t, r):
                act.wait_ge(up_done, UP0 + 2 * t + 1)
                act.wait_ge(hid_ready, HID0 + t - 1)
                act.activation(th[:, r % 2], ps[:, 1 + r % 2], ACT.Tanh, scale=0.5).then_inc(tanh_done, 1)

            def copy_hidden(t, r):
                act.wait_ge(ht_done, t + 1)
                act.wait_ge(down_done, DOWN0 + t - 1)
                act.copy(hT[:, r % 2].rearrange("p f t -> p (f t)"), ps[:, 5]).then_inc(hT_ready, 1)

            def routed_out(rt, r):
                act.wait_ge(down_done, DOWN0 + NTILE + rt + 1)
                act.wait_ge(add_turn, ADD0 + rt - 1)
                act.activation(yout[:, r % 2], ps[:, DOWN_BANK, 0:DM], ACT.Copy,
                               scale=xrow[:, r, DM + 1:DM + 2]).then_inc(yout_ready, 1)

            def step(t, r, todo):
                if todo >= 2:
                    tanh(t + 1, r + 1)
                copy_hidden(t, r)
                if todo >= 3:
                    copy_rows(t + 2, r + 2)

            copy_rows(0, 0)
            copy_rows(1, 1)
            tanh(0, 0)
            for t in range(NTILE):
                step(t, t % 4, 3)
                if t == 0:
                    columns_out(BATCH, "yt0")
                    columns_out(BATCH, "yt1")
                if t == 3:
                    store_rows(BATCH)
                    columns_out(BATCH, "rt0")
                    columns_out(BATCH, "rt1")
                if t == 4:
                    router_exp(BATCH)
            for r in range(2):
                act.wait_ge(row_out[r], ROWS_OUT)
            with act.Fori(0, (RTILES - 2) // 4) as i:
                for r in range(4):
                    step(NTILE + 4 * i + r, r, 3)
                    routed_out(4 * i + r, r)
            for rt in range((RTILES - 2) // 4 * 4, RTILES):
                step(NTILE + rt, rt % 4, min(3, RTILES - rt))
                routed_out(rt, rt % 4)

        @block.vector
        def _(dve):
            for s, n in ((split_rest, REST0), (split_low, LOW0), (value_ready, VAL0), (a_maxed, AMAX0),
                         (misc_free, MISC0), (hid_ready, HID0), (yout_ready, YO0)):
                dve.sem_inc(s, n)
            dve.memset(eps_c[:], EPS).then_inc(rstd_const, 1)
            dve.memset(minus_half[:], -0.5).then_inc(rstd_const, 1)
            dve.memset(key_ones(0), ONE_PAIR).then_inc(ones_rows, 1)
            def low_part(b, n):
                r = n % SPLIT_RING
                dve.wait_ge(split_rest, REST0 + NSPLIT * b + n + 1)
                if n in ACT_MIDS:
                    dve.wait_ge(split_mid_act, len(ACT_MIDS) * b + ACT_MIDS.index(n) + 1)
                else:
                    dve.wait_ge(split_mid, (NSPLIT - len(ACT_MIDS)) * b + n + 1 - sum(m < n for m in ACT_MIDS))
                dve.tensor_tensor(parts[:, r, 2], rest[:, n % 2], parts[:, r, 1], ALU.subtract).then_inc(split_low, 1)

            def normalize_x(b):
                dve.wait_ge(rstd_step, 2 * b + 2)
                dve.wait_ge(tr_done, TR0 + 3 * b - 1)
                for t in range(4):
                    dve.tensor_scalar(xn[:, t], xall[:, 4 * b + t], mv[:, 4 * b + t, 0:1], rstd[:, bass.ds(4 * b + t, 1)],
                                      ALU.subtract, ALU.mult).then_inc(xn_ready, 1)

            def projections_batch(b, last):
                n = m = 0
                for i, (kind, t, half) in enumerate(OUTPUTS):
                    if i == 4 and not last:
                        normalize_x(b + 1)
                    bank = ps[:, MM_BANK + i % MM_RING]
                    if kind == "value":
                        dve.wait_ge(mm_done, MM0 + len(OUTPUTS) * b + i + 1)
                        dve.tensor_tensor(V[:, b, 1 - t, 2 * half:2 * half + 2, :],
                                          bank.rearrange("p (t c) -> p t c", t=2),
                                          rowb[:, t:t + 1].to_broadcast([P, 2, DM]), ALU.add).then_inc(value_ready, 1)
                        m += 1
                    else:
                        dve.wait_ge(split_high, HIGH0 + 2 * (NSPLIT * b + n + 1))
                        dve.wait_ge(split_low, LOW0 + NSPLIT * b + n - 1)
                        dve.tensor_tensor(rest[:, n % 2], q32[:, n % 2], parts[:, n % SPLIT_RING, 0],
                                          ALU.subtract).then_inc(split_rest, 1)
                        if n:
                            low_part(b, n - 1)
                        n += 1
                low_part(b, NSPLIT - 1)

            def first_stats(c):
                dve.wait_ge(x_in[c], 16)
                for n in range(QT * c, QT * c + QT):
                    dve.bn_stats(stats[:, n], xall[:, n]).then_inc(stats_done, 1)
                for n in range(QT * c, QT * c + QT):
                    dve.wait_ge(stats_done, n + 1)
                    dve.bn_aggr(mv[:, n], stats[:, n]).then_inc(aggr_done, 1)

            first_stats(0)
            normalize_x(0)
            for c in range(1, BATCH):
                first_stats(c)
            dve.wait_ge(row_params_in, 16)
            with dve.Fori(0, BATCH - 1) as b:
                projections_batch(b, False)
            projections_batch(BATCH - 1, True)
            def unit_max(u, r, k):
                y, qt, pair, keys = a_unit(k)
                dve.wait_ge(a_scores, 16 * u + k + 1)
                slot = A_BANK + 2 * (k % 2)
                dve.tensor_reduce(maxes[:, r, y, 2 * pair:2 * pair + 2, qt], ps[:, slot:slot + 2, 0:keys], AX,
                                  ALU.max).then_inc(a_maxed, 1)

            def middle_rows(u, r):
                dve.wait_ge(mrow_high, u + 1)
                dve.scalar_tensor_tensor(out=mrow[:, r, 1], in0=ps[0:32, MISC_BANK, 0:P], scalar=-1.0, in1=mrow[:, r, 0],
                                         op0=ALU.mult, op1=ALU.subtract).then_inc(mrow_ready, 1)
                dve.wait_ge(mrow_ready, u + 1)
                dve.sem_inc(misc_free, 1)

            def normalize(u, y, number):
                dve.wait_ge(misc_ready, MR0 + number + 1)
                rows = ps[:, MISC_BANK].rearrange("p (q h c) -> p q h c", q=QT, h=G)
                done = 2 * u + (1 if y else 2)
                dve.reciprocal(recip[:, y], rows[:, :, :, HD]).then_inc(recip_done, 1)
                dve.wait_ge(recip_done, done)
                dve.wait_ge(y_added, YA0 + u)
                dve.tensor_tensor(ynorm[:, y], rows[:, :, :, 0:HD],
                                  recip[:, y].unsqueeze(3).to_broadcast([P, QT, G, HD]), ALU.mult).then_inc(ynorm_ready, 1)
                dve.wait_ge(ynorm_ready, done)
                dve.sem_inc(misc_free, 1)

            def residual(b, half):
                dve.wait_ge(misc_ready, MR0 + job(b, "prev", f"z{half}") + 1)
                dve.wait_ge(xb_ready, b)
                tiles = xall[:, bass.ds(QT * (b - 1) + 2 * half, 2)]
                dve.scalar_tensor_tensor(out=tiles, in0=ps[:, MISC_BANK].rearrange("p (t c) -> p t c", t=2),
                                         scalar=tanh_g[:, 0:1], in1=tiles, op0=ALU.mult, op1=ALU.add).then_inc(misc_free, 1)

            def second_stats(b):
                dve.wait_ge(misc_free, MISC0 + job(b, "prev", "z1") + 1)
                dve.sem_inc(dve_waited, 1)
                for t in range(QT):
                    dve.bn_stats(stats[:, t], xall[:, QT * (b - 1) + t]).then_inc(stats2_done, 1)
                for t in range(QT):
                    dve.wait_ge(stats2_done, QT * (b - 1) + t + 1)
                    dve.sem_inc(dve_waited, 1)
                    dve.bn_aggr(mv[:, t], stats[:, t]).then_inc(aggr2_done, 1)

            def second_rows(b, half):
                dve.wait_ge(v_staged, G * b)
                dve.wait_ge(rstd2_step, 2 * b)
                for t in range(2 * half, 2 * half + 2):
                    n = QT * (b - 1) + t
                    dve.tensor_scalar(xr[:, n, 0:DM] if b is BATCH else xstage[:, t], xall[:, n], mv[:, t, 0:1],
                                      rstd[:, t:t + 1], ALU.subtract, ALU.mult).then_inc(xr_ready, 1)

            def attention_batch(b, first, last):
                for g in range(G):
                    for v in range(8):
                        if not (last and g >= 2):
                            unit_max(G * b + g + 2, g % 2, 2 * v)
                            unit_max(G * b + g + 2, g % 2, 2 * v + 1)
                        if v == 1 and not (last and g == G - 1):
                            middle_rows(G * b + g + 1, (g + 1) % 2)
                        if v == 2 and g > 0:
                            normalize(G * b + g - 1, 0, job(b, "y", g - 1, 0))
                        elif v == 2 and not first:
                            normalize(G * b - 1, 0, job(b, "prev", "y"))
                        if v == 6:
                            normalize(G * b + g, 1, job(b, "y", g, 1))
                        if not first and g == 0 and v in (5, 7):
                            residual(b, (v - 5) // 2)
                        if not first and (g, v) == (1, 3):
                            second_stats(b)
                        if not first and g == 2 and v < 2:
                            second_rows(b, v)

            for u in range(2):
                for k in range(16):
                    unit_max(u, u, k)
                if u == 0:
                    middle_rows(0, 0)
            dve.wait_ge(tanh_ready, 1)
            dve.tensor_scalar(tbp[:], rowb[:, 2], tanh_g[:, 0:1], None, ALU.mult).then_inc(tbp_ready, 1)
            dve.tensor_scalar(ffn_c[:], tanh_g[:, 1:2], 0.5 / (1 + TOPK), None, ALU.mult).then_inc(ffn_c_ready, 1)

            attention_batch(0, True, False)
            with dve.Fori(1, BATCH - 1) as b:
                attention_batch(b, False, False)
            attention_batch(BATCH - 1, False, True)
            normalize(G * BATCH - 1, 0, job(BATCH, "prev", "y"))

            steps_done = [0]

            def chain(ins):
                steps_done[0] += 1
                ins.then_inc(route_step, 1)
                dve.wait_ge(route_step, steps_done[0])

            def over_e(t):
                return t.unsqueeze(2).to_broadcast([P, NTILE, EXPERTS])

            def choose():
                dve.wait_ge(route_const, 3)
                dve.wait_ge(misc_free, MISC0 + job(BATCH, "prev", "logits") + 1)
                order_bc = order_e.unsqueeze(1).to_broadcast([P, NTILE, EXPERTS])
                chain(dve.tensor_scalar(gate, expz[:], 1.0, None, ALU.add))
                chain(dve.reciprocal(gate, gate))
                chain(dve.tensor_reduce(best[:, :, 0], gate, AX, ALU.max))
                chain(dve.tensor_tensor(firstm, gate, over_e(best[:, :, 0]), ALU.is_equal))
                chain(dve.tensor_tensor(rankv, firstm, order_bc, ALU.mult))
                chain(dve.tensor_reduce(best[:, :, 1], rankv, AX, ALU.max))
                chain(dve.tensor_tensor(top1, rankv, over_e(best[:, :, 1]), ALU.is_equal))
                chain(dve.scalar_tensor_tensor(out=pick, in0=top1, scalar=-2.0, in1=gate, op0=ALU.mult, op1=ALU.add))
                chain(dve.tensor_reduce(best[:, :, 2], pick, AX, ALU.max))
                chain(dve.tensor_tensor(firstm, pick, over_e(best[:, :, 2]), ALU.is_equal))
                chain(dve.tensor_tensor(rankv, firstm, order_bc, ALU.mult))
                chain(dve.tensor_reduce(best[:, :, 3], rankv, AX, ALU.max))
                chain(dve.tensor_tensor(top2, rankv, over_e(best[:, :, 3]), ALU.is_equal))
                dve.tensor_tensor(chosen_b, top1.rearrange("p n e -> p e n"), top2.rearrange("p n e -> p e n"),
                                  ALU.add).then_inc(chosen_ready, 1)
                chain(dve.tensor_tensor(gsum, best[:, :, 0], best[:, :, 2], ALU.add))
                chain(dve.reciprocal(ginv, gsum))
                dve.wait_ge(ffn_c_ready, 1)
                for k in range(2):
                    chain(dve.scalar_tensor_tensor(out=wts[:, k], in0=best[:, :, 2 * k], scalar=ffn_c[:, 0:1], in1=ginv,
                                                   op0=ALU.mult, op1=ALU.mult))

            def assign_slots():
                dve.wait_ge(counts_done, 1)
                earlier = ps[:, 7, 0:NE]
                totals = ps[:, 7, NE:2 * NE]
                chain(dve.tensor_tensor_scan(run_tot, restart, totals, 0.0, ALU.mult, ALU.add))
                run_en = run_tot.rearrange("p (e n) -> p e n", e=EXPERTS)
                chain(dve.tensor_tensor(over, run_en[:, :, NTILE - 1:NTILE].to_broadcast([P, EXPERTS, NTILE]),
                                        steps.unsqueeze(1).to_broadcast([P, EXPERTS, NTILE]), ALU.is_gt))
                chain(dve.tensor_reduce(ntiles, over, AX, ALU.add))
                chain(dve.tensor_tensor_scan(ends, ones_e, ntiles, 0.0, ALU.mult, ALU.add))
                chain(dve.tensor_tensor(passed, tile_no.unsqueeze(2).to_broadcast([P, RTILES, EXPERTS]),
                                        ends.unsqueeze(1).to_broadcast([P, RTILES, EXPERTS]), ALU.is_ge))
                chain(dve.tensor_reduce(emap_f, passed, AX, ALU.add))
                dve.tensor_scalar(emap, emap_f, float(EXPERTS - 1), None, ALU.min).then_inc(emap_ready, 1)
                chain(dve.tensor_tensor(starts, ends, ntiles, ALU.subtract))
                chain(dve.tensor_tensor(slot_en, run_tot, totals, ALU.subtract))
                chain(dve.tensor_tensor(slot_en, slot_en, earlier, ALU.add))
                slot_v = slot_en.rearrange("p (e n) -> p e n", e=EXPERTS)
                chain(dve.scalar_tensor_tensor(out=slot_e, in0=starts.unsqueeze(2).to_broadcast([P, EXPERTS, NTILE]),
                                               scalar=float(P), in1=slot_v, op0=ALU.mult, op1=ALU.add))
                for k, top in enumerate((top1, top2)):
                    chain(dve.tensor_tensor(pick, top, slot_e.rearrange("p e n -> p n e"), ALU.mult))
                    chain(dve.tensor_reduce(slot_f[:, k], pick, AX, ALU.add))
                    dve.tensor_copy(slot_i[:, k], slot_f[:, k]).then_inc(slots_ready, 1)

            def hidden(t, r):
                a, b_ = ps[:, 1 + r % 2], ps[:, 3 + r % 2]
                dve.wait_ge(tanh_done, t + 1)
                dve.scalar_tensor_tensor(out=gated[:, r % 2], in0=th[:, r % 2], scalar=1.0, in1=a, op0=ALU.add,
                                         op1=ALU.mult).then_inc(gated_ready, 1)
                dve.wait_ge(gated_ready, t + 1)
                dve.wait_ge(up_done, UP0 + 2 * t + 2)
                dve.tensor_tensor(hid[:, r % 2], gated[:, r % 2], b_, ALU.mult).then_inc(hid_ready, 1)

            def shared_out(t, r):
                dve.wait_ge(down_done, DOWN0 + t + 1)
                if t >= 2:
                    dve.wait_ge(row_out[t % 2], 16 * (t // 2))
                dve.scalar_tensor_tensor(out=yout[:, r % 2], in0=ps[:, DOWN_BANK, 0:DM], scalar=ffn_c[:, 0:1],
                                         in1=xall[:, t], op0=ALU.mult, op1=ALU.add).then_inc(yout_ready, 1)

            hidden(0, 0)
            for t in range(NTILE):
                hidden(t + 1, t + 1)
                if t == 1:
                    residual(BATCH, 0)
                shared_out(t, t)
                if t == 1:
                    residual(BATCH, 1)
                    second_stats(BATCH)
                if t == 2:
                    second_rows(BATCH, 0)
                    second_rows(BATCH, 1)
                if t == 4:
                    choose()
                if t == 5:
                    assign_slots()
            with dve.Fori(0, (RTILES - 2) // 4) as i:
                for r in range(4):
                    hidden(NTILE + 4 * i + r + 1, r + 1)
            for rt in range((RTILES - 2) // 4 * 4 + 1, RTILES):
                hidden(NTILE + rt, rt % 4)

        @block.gpsimd
        def _(pool):
            for s, n in ((y_added, YA0), (add_turn, ADD0)):
                pool.sem_inc(s, n)
            pool.memset(ident[:], 0.0).then_inc(consts_ready, 1)
            pool.memset(causal[:], 0.0).then_inc(consts_ready, 1)
            pool.memset(before[:], 0.0).then_inc(consts_ready, 1)
            pool.memset(ones_b[:], 1.0).then_inc(consts_ready, 1)
            pool.memset(pad[:], 0.0).then_inc(consts_ready, 1)
            pool.wait_ge(consts_ready, 5)
            pool.affine_select(out=ident[:], in_=ident[:], compare_op=ALU.not_equal, fill=1.0, base=0,
                               pattern=[[-1, P]], channel_multiplier=1).then_inc(consts_ready, 1)
            pool.affine_select(out=causal[:], in_=causal[:], compare_op=ALU.is_ge, fill=NEG, base=0,
                               pattern=[[-1, P]], channel_multiplier=1).then_inc(consts_ready, 1)
            pool.affine_select(out=before[:], in_=before[:], compare_op=ALU.is_ge, fill=1.0, base=0,
                               pattern=[[-1, P]], channel_multiplier=1).then_inc(consts_ready, 1)
            pool.wait_ge(consts_ready, 8)
            for dst, src in ((ident_b, ident), (causal_b, causal), (before_b, before)):
                pool.tensor_scalar(dst[:], src[:], 1.0, None, ALU.mult).then_inc(consts_ready, 1)
            pool.iota(pad[:, DM:DM + 1].bitcast(I32), pattern=[[0, 1]], base=TOK, channel_multiplier=1).then_inc(pad_ready, 1)

            pool.wait_ge(rstd_const, 2)

            def alone():
                pool.sem_inc(pool_waited, 1)

            for c in range(BATCH):
                pool.wait_ge(aggr_done, 4 * (c + 1))
                pool.tensor_tensor(rstd[:, 4 * c:4 * c + 4], mv[:, 4 * c:4 * c + 4, 1],
                                   eps_c[:].to_broadcast([P, 4]), ALU.add).then_inc(rstd_step, 1)
                pool.wait_ge(rstd_step, 2 * c + 1)
                pool.tensor_tensor(rstd[:, 4 * c:4 * c + 4], rstd[:, 4 * c:4 * c + 4],
                                   minus_half[:].to_broadcast([P, 4]), ALU.pow).then_inc(rstd_step, 1)

            pool.wait_ge(ctx_loaded, 16)
            with pool.Fori(0, BATCH) as b:
                pool.wait_ge(tr_done, TR0 + 3 * b)
                pool.tensor_copy(ctx_b, ctx_sb[:, bass.ds(4 * b, 4)]).then_inc(ctx_staged, 1)
                for n in range(NSPLIT):
                    if n in ACT_MIDS:
                        continue
                    pool.wait_ge(split_rest, REST0 + NSPLIT * b + n + 1)
                    alone()
                    pool.tensor_scalar(parts[:, n % SPLIT_RING, 1], rest[:, n % 2], 1.0, None,
                                       ALU.mult).then_inc(split_mid, 1)

            pool.wait_ge(split_mid, BATCH * (NSPLIT - len(ACT_MIDS)))
            pool.memset(key_ones(1), ONE_PAIR).then_inc(ones_rows, 1)
            pool.wait_ge(ones_rows, 2)
            pool.wait_ge(mm_done, MM0 + BATCH * len(OUTPUTS))
            pool.memset(vaug, 0.0).then_inc(vaug_clear, 1)
            pool.wait_ge(vaug_clear, 1)
            pool.memset(vaug[:, :, :, :, HD:HD + 1], 1.0).then_inc(vaug_clear, 1)
            pool.wait_ge(vaug_clear, 2)
            pool.wait_ge(value_ready, VAL0 + BATCH * NVALUE)

            def add_types(b, g):
                u = G * b + g
                pool.wait_ge(ynorm_ready, 2 * u + 2)
                if g == 0 and not (isinstance(b, int) and b == 0):
                    pool.wait_ge(misc_ready, MR0 + job(b, "prev", "yt1") + 1)
                cols = Y[:, :, G * HD * g:G * HD * (g + 1)].rearrange("p q (h d) -> p q h d", h=G)
                pool.tensor_tensor(cols, ynorm[:, 0], ynorm[:, 1], ALU.add).then_inc(y_added, 1)

            def second_rstd(b):
                pool.wait_ge(aggr2_done, QT * b)
                alone()
                r_b = rstd[:, 0:QT]
                pool.tensor_tensor(r_b, mv[:, 0:QT, 1], eps_c[:].to_broadcast([P, QT]),
                                   ALU.add).then_inc(rstd2_step, 1)
                pool.wait_ge(rstd2_step, 2 * b - 1)
                alone()
                pool.tensor_tensor(r_b, r_b, minus_half[:].to_broadcast([P, QT]), ALU.pow).then_inc(rstd2_step, 1)

            def stage_values(b, g):
                pool.wait_ge(av_done, AV0 + 8 * (G * b + g) - 8)
                pool.tensor_copy(vaug[:, g % 2, :, :, 0:HD], V[:, b, :, :, G * HD * g:G * HD * (g + 1)].rearrange(
                    "p y j (h d) -> p (y j) h d", h=G)).then_inc(v_staged, 1)

            def attention_batch(b, first, last):
                for g in range(G):
                    u = G * b + g
                    if g > 0:
                        add_types(b, g - 1)
                    elif not first:
                        add_types(b - 1, G - 1)
                    if g == 1:
                        if first:
                            pool.wait_ge(tbp_ready, 1)
                        tiles = xall[:, bass.ds(4 * b, 4)]
                        pool.tensor_tensor(tiles, tiles, tbp[:].unsqueeze(1).to_broadcast([P, 4, DM]),
                                           ALU.add).then_inc(xb_ready, 1)
                    if not (last and g == G - 1):
                        stage_values(b + (g + 1) // G, (g + 1) % G)
                    if g == 3 and not first:
                        pool.wait_ge(xr_ready, QT * b)
                        pool.wait_ge(shared_in, 16 * b)
                        pool.tensor_copy(xr[:, bass.ds(QT * (b - 1), QT), 0:DM], xstage).then_inc(xr_kept, 1)
                    for v in range(4, 8):
                        _y, j, q0 = key_tile(v)
                        pool.wait_ge(exp_done, EXP0 + 4 * (8 * u + v) + 4)
                        alone()
                        diag = prob[:, v % 4, :, q0:q0 + P]
                        pool.affine_select(out=diag, in_=diag, compare_op=ALU.is_ge, fill=0.0, base=0,
                                           pattern=[[0, G], [1, P]], channel_multiplier=-1).then_inc(masked, 1)
                    if g == 1 and not first:
                        second_rstd(b)

            stage_values(0, 0)
            attention_batch(0, True, False)
            with pool.Fori(1, BATCH - 1) as b:
                attention_batch(b, False, False)
            attention_batch(BATCH - 1, False, True)
            add_types(BATCH - 1, G - 1)

            pool.iota(consts_i, pattern=[[1, NC_I]], base=0, channel_multiplier=0).then_inc(route_const, 1)
            pool.iota(tok_i, pattern=[[P, NTILE]], base=0, channel_multiplier=1).then_inc(route_const, 1)
            pool.wait_ge(route_const, 2)
            pool.tensor_scalar(order_e, consts_i[:, 0:EXPERTS], -1.0, float(EXPERTS), ALU.mult, ALU.add).then_inc(row_tail, 1)
            pool.tensor_scalar(steps, consts_i[:, 0:NTILE], float(P), None, ALU.mult).then_inc(row_tail, 1)
            pool.tensor_scalar(tile_no, consts_i[:, 0:RTILES], 1.0, None, ALU.mult).then_inc(row_tail, 1)
            pool.memset(ones_e, 1.0).then_inc(row_tail, 1)
            pool.memset(restart, 1.0).then_inc(row_tail, 1)
            pool.wait_ge(row_tail, 5)
            pool.memset(restart.rearrange("p (e n) -> p e n", e=EXPERTS)[:, :, 0:1], 0.0).then_inc(route_const, 1)

            second_rstd(BATCH)

            pool.wait_ge(slots_ready, 1)
            pool.wait_ge(xr_ready, NTILE)
            pool.wait_ge(xr_kept, BATCH - 1)
            pool.wait_ge(pad_out, 16 * (BATCH - 1))
            pool.tensor_copy(xr[:, :, DM].bitcast(I32), tok_i).then_inc(row_tail, 1)
            for k in range(2):
                pool.wait_ge(slots_ready, k + 1)
                if k:
                    pool.wait_ge(scattered, 16 * NTILE)
                pool.tensor_copy(xr[:, :, DM + 1], wts[:, k]).then_inc(row_tail, 1)
                pool.wait_ge(row_tail, 7 + k)
                for n in range(NTILE):
                    pool.indirect_dma_start(out=routed_rows[:, :], out_offset=bass.IndirectOffsetOnAxis(
                        ap=slot_i[:, k, n:n + 1].bitcast(mybir.dt.uint32), axis=0), in_=xr[:, n, :], in_offset=None).then_inc(scattered, 16)

            for r in range(2):
                pool.wait_ge(row_out[r], ROWS_OUT)
            pool.wait_ge(dummy_out, 16)

            def add_rows(rt, r):
                pool.wait_ge(yout_ready, YO0 + NTILE + rt + 1)
                alone()
                pool.indirect_dma_start(out=out[:, :], out_offset=bass.IndirectOffsetOnAxis(
                    ap=xrow[:, r, DM:DM + 1].bitcast(mybir.dt.uint32), axis=0), in_=yout[:, r % 2], in_offset=None,
                    compute_op=ALU.add).then_inc(row_added, 16)
                pool.wait_ge(row_added, 16 * (rt + 1))
                pool.sem_inc(add_turn, 1)

            with pool.Fori(0, RTILES // 4) as i:
                for r in range(4):
                    add_rows(4 * i + r, r)
            for rt in range(RTILES // 4 * 4, RTILES):
                add_rows(rt, rt % 4)

        @block.tensor
        def _(pe):
            for s, n in ((tr_done, TR0), (mm_done, MM0), (misc_ready, MR0), (av_done, AV0),
                         (up_done, UP0), (down_done, DOWN0)):
                pe.sem_inc(s, n)
            pe.wait_ge(consts_ready, 11)

            def to_columns(b, k):
                pe.wait_ge(trT_ready, TRT0 + 3 * b + k - 2)
                src = xn if k < 2 else ctx_b
                for t in range(QT):
                    mm = pe.transpose(ps[:, TR_BANK[k], P * t:P * t + P], src[:, t, P * (k % 2):P * (k % 2) + P], ident[:])
                mm.then_inc(tr_done, 1)

            WEIGHT_ORDER = [("split", 0), ("split", 1), ("split", 2), ("value", 0), ("split", 3)]
            SPLITS = [i for i, o in enumerate(OUTPUTS) if o[0] == "split"]
            VALUES = [i for i, o in enumerate(OUTPUTS) if o[0] == "value"]

            def x_to_columns(b):
                pe.wait_ge(xn_ready, 4 * b + 4)
                to_columns(b, 0)
                to_columns(b, 1)

            def projections_batch(b, last):
                for i, (kind, t, half) in enumerate(OUTPUTS):
                    if i == 4:
                        pe.wait_ge(ctx_staged, b + 1)
                        to_columns(b, 2)
                    if i == 0:
                        pe.wait_ge(trT_ready, TRT0 + 3 * b + 2)
                    if i == 8:
                        if not last:
                            x_to_columns(b + 1)
                        pe.wait_ge(trT_ready, TRT0 + 3 * b + 3)
                    if (kind, t) in WEIGHT_ORDER:
                        pe.wait_ge(proj_in[WEIGHT_ORDER.index((kind, t))], 16)
                    before_i, bb = (i - MM_RING, b) if i >= MM_RING else (i - MM_RING + len(OUTPUTS), b - 1)
                    if before_i in SPLITS:
                        pe.wait_ge(split_high, HIGH0 + 2 * (NSPLIT * bb + SPLITS.index(before_i) + 1))
                    else:
                        pe.wait_ge(value_ready, VAL0 + NVALUE * bb + VALUES.index(before_i) + 1)
                    bank = ps[:, MM_BANK + i % MM_RING]
                    if kind == "split" and t < 3:
                        for k in range(KT):
                            mm = pe.matmul(bank, wproj[:, t, k, P * half:P * half + P], xnT[:, k], start=k == 0, stop=k == KT - 1)
                    elif kind == "split":
                        mm = pe.matmul(bank, wcross[:, 0, P * half:P * half + P], ctxT, start=True, stop=True)
                    else:
                        for s in range(2):
                            tok = slice(P * (2 * half + s), P * (2 * half + s) + P)
                            dst = bank[:, DM * s:DM * s + DM]
                            if t == 0:
                                for k in range(KT):
                                    mm = pe.matmul(dst, xnT[:, k, tok], wproj[:, 3, k], start=k == 0, stop=k == KT - 1)
                            else:
                                mm = pe.matmul(dst, ctxT[:, tok], wcross[:, 1], start=True, stop=True)
                    mm.then_inc(mm_done, 1)

            x_to_columns(0)
            with pe.Fori(0, BATCH - 1) as b:
                projections_batch(b, False)
            projections_batch(BATCH - 1, True)
            pe.wait_ge(late_in, 32)

            def score_unit(u, b, g, k):
                y, qt, pair, keys = a_unit(k)
                pe.wait_ge(a_maxed, AMAX0 + 16 * u + k - 1)
                slot = A_BANK + 2 * (k % 2)
                for s in range(2):
                    h = 2 * pair + s
                    mm = pe.matmul(ps[:, slot + s, 0:keys], stk[0:ROWS, g, 2 * y, h, P * qt:P * qt + P],
                                   stk[0:ROWS, g, 2 * y + 1, h, 0:keys], start=True, stop=bool(y))
                    if not y:
                        mm = pe.matmul(ps[:, slot + s, keys - P:keys], ident_b[:], causal_b[:], start=False, stop=True)
                mm.then_inc(a_scores, 1)

            def key_scores(b, g, v, h):
                y, j, q0 = key_tile(v)
                bank, ring = b_bank(b, g, h)
                if (g, v) == (2, 0):
                    ring = 2
                    if bank == A_BANK:
                        pe.wait_ge(a_maxed, AMAX0 + 16 * G * BATCH)
                pe.wait_ge(exp_done, EXP0 + 4 * (8 * (G * b + g) + v) + h + 1 - ring)
                pe.matmul(ps[:, bank, q0:SEQ], stk[0:STACKED, g, 2 * y + 1, h, P * j:P * j + P],
                          stk[0:STACKED, g, 2 * y, h, q0:SEQ], start=True, stop=True).then_inc(b_scores, 1)

            def times_values(b, g, v):
                y, j, q0 = key_tile(v)
                u = G * b + g
                if v == 0:
                    pe.wait_ge(v_staged, u + 1)
                if j == 0:
                    pe.wait_ge(o_copied, OC0 + 2 * u + (0 if y else 1))
                pe.wait_ge(exp_done, EXP0 + 4 * (8 * u + v) + 4)
                if not y:
                    pe.wait_ge(masked, 4 * u + j + 1)
                for h in range(G):
                    mm = pe.matmul(ps[32 * h:32 * h + 32, O_BANK, q0:SEQ], vaug[:, g % 2, v, h], prob[:, v % 4, h, q0:SEQ],
                                   start=j == 0, stop=j == QT - 1)
                mm.then_inc(av_done, 1)

            def max_to_rows(u, r, wait_job):
                pe.wait_ge(a_maxed, AMAX0 + 16 * u + 16)
                pe.wait_ge(misc_free, MISC0 + wait_job)
                pe.transpose(ps[0:32, MISC_BANK, 0:P], maxes[:, r].rearrange("p y h q -> p (y h q)"),
                             ident[:]).then_inc(misc_ready, 1)

            def o_to_rows(u, y, number):
                pe.wait_ge(o_copied, OC0 + 2 * u + (1 if y else 2))
                pe.wait_ge(misc_free, MISC0 + number)
                for t in range(QT):
                    mm = pe.transpose(ps[:, MISC_BANK, P * t:P * t + P], osb[:, y, P * t:P * t + P], ident[:])
                mm.then_inc(misc_ready, 1)

            def y_to_columns(b, k):
                pe.wait_ge(y_added, YA0 + G * b)
                pe.wait_ge(misc_free, MISC0 + job(b, "prev", f"yt{k}"))
                for t in range(QT):
                    mm = pe.transpose(ps[:, MISC_BANK, P * t:P * t + P], Y[:, t, P * k:P * k + P], ident[:])
                mm.then_inc(misc_ready, 1)

            def project_out(b, half):
                pe.wait_ge(misc_free, MISC0 + job(b, "prev", f"z{half}"))
                for t in range(2):
                    tok = slice(P * (2 * half + t), P * (2 * half + t) + P)
                    for k in range(KT):
                        mm = pe.matmul(ps[:, MISC_BANK, DM * t:DM * t + DM], YT[:, k, tok], wp_sb[:, k],
                                       start=k == 0, stop=k == KT - 1)
                mm.then_inc(misc_ready, 1)

            def normed_to_columns(b, k):
                pe.wait_ge(xr_ready, QT * b)
                pe.wait_ge(misc_free, MISC0 + job(b, "prev", f"rt{k}"))
                for t in range(QT):
                    rows = (xr[:, NTILE - QT + t] if b is BATCH else xstage[:, t])[:, P * k:P * k + P]
                    mm = pe.transpose(ps[:, MISC_BANK, P * t:P * t + P], rows, ident[:])
                mm.then_inc(misc_ready, 1)

            def router(b):
                pe.wait_ge(misc_free, MISC0 + job(b, "prev", "logits"))
                for t in range(QT):
                    for k in range(KT):
                        mm = pe.matmul(ps[:, MISC_BANK, EXPERTS * t:EXPERTS * t + EXPERTS], YT[:, k, P * t:P * t + P],
                                       wg_sb[:, k], start=k == 0, stop=k == KT - 1)
                mm.then_inc(misc_ready, 1)

            def attention_batch(b, first, last):
                for g in range(G):
                    ahead_g, ahead_b = (g + 2) % G, b + (g + 2) // G
                    pe.wait_ge(stack_in[g], STACK_DMAS * (b + 1))
                    pe.wait_ge(max_in[g], 32 * (b + 1))
                    if not (last and g >= 2):
                        pe.wait_ge(stack_in[ahead_g], STACK_DMAS * (ahead_b + 1))
                    for v in range(8):
                        key_scores(b, g, v, 0)
                        if not (last and g >= 2):
                            score_unit(G * b + g + 2, ahead_b, ahead_g, 2 * v)
                        key_scores(b, g, v, 1)
                        if v >= 2:
                            times_values(b, g, v - 2)
                        elif g > 0:
                            times_values(b, g - 1, 6 + v)
                        elif not first:
                            times_values(b - 1, G - 1, 6 + v)
                        key_scores(b, g, v, 2)
                        if not (last and g >= 2):
                            score_unit(G * b + g + 2, ahead_b, ahead_g, 2 * v + 1)
                        key_scores(b, g, v, 3)
                        if v == 1 and not (last and g == G - 1):
                            max_to_rows(G * b + g + 1, (g + 1) % 2, job(b, "max", g))
                        if v == 2 and g > 0:
                            o_to_rows(G * b + g - 1, 0, job(b, "y", g - 1, 0))
                        elif v == 2 and not first:
                            o_to_rows(G * b - 1, 0, job(b, "prev", "y"))
                        if v == 6:
                            o_to_rows(G * b + g, 1, job(b, "y", g, 1))
                        if not first and g == 0:
                            if v in (3, 4):
                                y_to_columns(b, v - 3)
                            if v in (5, 7):
                                project_out(b, (v - 5) // 2)
                        if not first and g == 2:
                            if v in (3, 4):
                                normed_to_columns(b, v - 3)
                            if v == 5:
                                router(b)

            for u in range(2):
                pe.wait_ge(stack_in[u], STACK_DMAS)
                for k in range(16):
                    score_unit(u, 0, u, k)
                if u == 0:
                    max_to_rows(0, 0, 0)
            pe.wait_ge(ones_rows, 2)
            attention_batch(0, True, False)
            with pe.Fori(1, BATCH - 1) as b:
                attention_batch(b, False, False)
            attention_batch(BATCH - 1, False, True)
            times_values(BATCH - 1, G - 1, 6)
            times_values(BATCH - 1, G - 1, 7)
            o_to_rows(G * BATCH - 1, 0, job(BATCH, "prev", "y"))

            def rows_to_columns(t, r, turn):
                pe.wait_ge(row_in[r], 16 * turn)
                pe.wait_ge(xT_ready, XT0 + t)
                for k in range(KT):
                    mm = pe.transpose(ps[:, 0, P * k:P * k + P], xrow[:, r, P * k:P * k + P], ident[:])
                mm.then_inc(xt_done, 1)

            def up(t, r, e, turn_hidden=None):
                pe.wait_ge(xT_ready, XT0 + t + 1)
                pe.wait_ge(hid_ready, HID0 + t - 1)
                for m in range(2):
                    if m and turn_hidden:
                        turn_hidden()
                    for k in range(KT):
                        mm = pe.matmul(ps[:, 1 + 2 * m + r % 2], xT[:, r % 2, k], w13[:, e, m, k], start=k == 0, stop=k == KT - 1)
                    mm.then_inc(up_done, 1)

            def hidden_to_columns(t, r):
                pe.wait_ge(hid_ready, HID0 + t + 1)
                pe.wait_ge(hT_ready, HT0 + t)
                for f in range(FT):
                    mm = pe.transpose(ps[:, 5, P * f:P * f + P], hid[:, r % 2, P * f:P * f + P], ident[:])
                mm.then_inc(ht_done, 1)

            def down(t, r, e):
                pe.wait_ge(hT_ready, HT0 + t + 1)
                pe.wait_ge(yout_ready, YO0 + t)
                for f in range(FT):
                    mm = pe.matmul(ps[:, DOWN_BANK, 0:DM], hT[:, r % 2, f], w2[:, e, f], start=f == 0, stop=f == FT - 1)
                mm.then_inc(down_done, 1)

            pe.wait_ge(shared_w_in, 16 * 3)
            rows_to_columns(0, 0, 1)
            rows_to_columns(1, 1, 1)
            up(0, 0, EXPERTS)
            for t in range(NTILE):
                if t + 1 < NTILE:
                    up(t + 1, t + 1, EXPERTS, lambda: hidden_to_columns(t, t))
                else:
                    pe.wait_ge(emap_ready, 1)
                    pe.wait_ge(expert_w_in, 16 * 3 * EXPERTS)
                    first = pe.value_load(emap[0:1, 0:1], min_val=0, max_val=EXPERTS - 1)
                    up(t + 1, t + 1, first, lambda: hidden_to_columns(t, t))
                rows_to_columns(t + 2, (t + 2) % 4, (t + 2) // 4 + 1)
                if t == 0:
                    y_to_columns(BATCH, 0)
                if t == 1:
                    project_out(BATCH, 0)
                if t == 3:
                    normed_to_columns(BATCH, 0)
                if t == 4:
                    router(BATCH)
                down(t, t, EXPERTS)
                if t == 0:
                    y_to_columns(BATCH, 1)
                if t == 1:
                    project_out(BATCH, 1)
                if t == 3:
                    normed_to_columns(BATCH, 1)
                if t == 5:
                    pe.wait_ge(chosen_ready, 1)
                    flat = chosen_b.rearrange("p e n -> p (e n)")
                    pe.matmul(ps[:, MISC_BANK, 0:NE], before_b[:], flat, start=True, stop=True)
                    pe.matmul(ps[:, MISC_BANK, NE:2 * NE], ones_b[:], flat, start=True, stop=True).then_inc(counts_done, 1)
            turns = NTILE // 4

            def expert(rt):
                return pe.value_load(emap[0:1, bass.ds(rt, 1)], min_val=0, max_val=EXPERTS - 1)

            with pe.Fori(0, (RTILES - 2) // 4) as i:
                this = expert(4 * i)
                for r in range(4):
                    rt = 4 * i + r
                    after = expert(rt + 1)
                    up(NTILE + rt + 1, r + 1, after, lambda: hidden_to_columns(NTILE + rt, r))
                    rows_to_columns(NTILE + rt + 2, (r + 2) % 4, turns + i + 1 + (r + 2) // 4)
                    down(NTILE + rt, r, this)
                    this = after
            for rt in range((RTILES - 2) // 4 * 4, RTILES):
                if rt + 1 < RTILES:
                    up(NTILE + rt + 1, rt + 1, expert(rt + 1), lambda: hidden_to_columns(NTILE + rt, rt))
                else:
                    hidden_to_columns(NTILE + rt, rt)
                if rt + 2 < RTILES:
                    rows_to_columns(NTILE + rt + 2, (rt + 2) % 4, turns + (rt + 2) // 4 + 1)
                down(NTILE + rt, rt, expert(rt))


def _layout(inputs):
    import numpy as np

    a = {name: np.asarray(v) for name, v in inputs.items()}

    def attn(name):
        return a["L0_xattn_" + name]

    def by_dim(w):
        return w.reshape(w.shape[:-1] + (HEADS, HD)).swapaxes(-1, -2).reshape(w.shape)

    def rows(w):
        return w.reshape(-1, P, w.shape[-1]).transpose(1, 0, 2)

    arrays = {
        "x": a["x"].reshape(TOK, DM),
        "ctx": a["ctx_512"].reshape(TOK, DC),
        "w_proj": np.stack([rows(by_dim(attn("Wq"))), rows(by_dim(attn("Wk"))), rows(by_dim(attn("Wcq"))),
                            rows(attn("Wv"))], 1),
        "w_cross": np.stack([by_dim(attn("Wck")), attn("Wcv")], 1),
        "w_out": rows(attn("Wp")),
        "part_bias": np.stack([by_dim(attn(n)).reshape(KT, P).T for n in ("bq", "bk", "bcq", "bck")], 1),
        "row_params": np.concatenate([attn("bv"), attn("bcv"), attn("bp"), a["g_xattn"], a["g_ffn"]]),
    }
    for name in ("Wg", "Ws1", "Ws3", "Ws2", "We1", "We3", "We2"):
        arrays[name] = a["L0_ffn_" + name]
    return {name: np.ascontiguousarray(v) for name, v in arrays.items()}


def kernel(**inputs):
    import numpy as np
    import concourse.bacc as bacc
    from concourse.bass_utils import run_bass_kernel_spmd

    nc = bacc.Bacc("TRN2", target_bir_lowering=False, num_devices=1)
    arrays, args = {}, []
    for name, a in _layout(inputs).items():
        arrays[f"in_{name}"] = a
        args.append(nc.dram_tensor(f"in_{name}", a.shape, mybir.dt.from_np(a.dtype), kind="ExternalInput").ap())
    args.append(nc.dram_tensor("out_0", (TOK + P, DM), F32, kind="ExternalOutput").ap())
    build(nc, *args)
    r = run_bass_kernel_spmd(nc, [arrays], core_ids=[0])
    return r.results[0]["out_0"][:TOK].reshape(BATCH, SEQ, DM)
```
